# Optimizing a Trainium2 kernel written in Bass

```python
import numpy as np
import jax
import jax.numpy as jnp

def _softmax(x, axis=-1):
    return jax.nn.softmax(x, axis=axis)

def _gelu(x):
    return jax.nn.gelu(x, approximate=True)

def _silu(x):
    return jax.nn.silu(x)

def _sigmoid(x):
    return jax.nn.sigmoid(x)

def _layernorm(x, axis=-1, eps=1e-05):
    m = jnp.mean(x, axis=axis, keepdims=True)
    v = jnp.var(x, axis=axis, keepdims=True)
    return (x - m) / jnp.sqrt(v + eps)

def _scatter_add(tgt, idx, src, axis=0):
    return tgt.at[idx].add(src)

def _segment_sum(src, seg, n):
    return jax.ops.segment_sum(src, seg, n)
kernel_name = 'mk_xattn_seq_d1_seqx_r4_74084b'

def setup_inputs(seed: int=0):
    np.random.seed(seed)
    _w = jnp.asarray

    def _rec_inputs():
        import jax
        import jax.numpy as jnp
        _rk = jax.random.key(seed)
        x = -0.0002928 + 1 * jax.random.normal(jax.random.fold_in(_rk, 1), (2, 512, 256), jnp.float32)
        _lenS = 512 - jax.random.randint(jax.random.fold_in(_rk, 7), (2,), 0, max(1, 512 // 4) + 1, jnp.int32)
        _lenS2 = 1024 - jax.random.randint(jax.random.fold_in(_rk, 8), (2,), 0, max(1, 1024 // 4) + 1, jnp.int32)
        _ctx_1024P = jax.random.normal(jax.random.fold_in(_rk, 11), (2, 16, 256), jnp.float32)
        _ctx_1024c = jax.random.dirichlet(jax.random.fold_in(_rk, 511), 0.3 * jnp.ones((16,), jnp.float32), (2, 1024))
        _ctx_1024t = jnp.einsum('bsk,bkd->bsd', _ctx_1024c, _ctx_1024P)
        _ctx_1024t = _ctx_1024t * jax.lax.rsqrt(jnp.mean(jnp.square(_ctx_1024t)) + 1e-12) * 0.953939
        ctx_1024 = -1.39393e-06 + 0.999914 * (_ctx_1024t + 0.3 * jax.random.normal(jax.random.fold_in(_rk, 611), (2, 1024, 256), jnp.float32))
        return (x, ctx_1024)
    x, ctx_1024 = _rec_inputs()

    def _L0_xattn_setup():
        import jax, jax.numpy as jnp
        import numpy as np
        B, Q, KV = (2, 512, 512)
        D_MODEL = 256
        N_HEADS = 16
        D_KV = 64
        EPS = 1e-06
        key = jax.random.key(seed)
        ks = jax.random.split(key, 7)
        s = 0.02
        return {'hidden_states': jax.random.normal(ks[0], (B, Q, D_MODEL), jnp.float32), 'key_value_states': jax.random.normal(ks[1], (B, KV, D_MODEL), jnp.float32), 'wq': jax.random.normal(ks[2], (D_MODEL, N_HEADS * D_KV), jnp.float32) * s, 'wk': jax.random.normal(ks[3], (D_MODEL, N_HEADS * D_KV), jnp.float32) * s, 'wv': jax.random.normal(ks[4], (D_MODEL, N_HEADS * D_KV), jnp.float32) * s, 'wo': jax.random.normal(ks[5], (N_HEADS * D_KV, D_MODEL), jnp.float32) * s, 'norm_w': jnp.ones((D_MODEL,), jnp.float32)}
    _L0_xattn_all = _L0_xattn_setup()
    _L0_xattn_in = {k: v for k, v in _L0_xattn_all.items() if k in ('wq', 'wk', 'wv', 'wo', 'norm_w')}
    del _L0_xattn_all
    return {'x': x, 'ctx_1024': ctx_1024, 'L0_xattn_wq': _L0_xattn_in['wq'], 'L0_xattn_wk': _L0_xattn_in['wk'], 'L0_xattn_wv': _L0_xattn_in['wv'], 'L0_xattn_wo': _L0_xattn_in['wo'], 'L0_xattn_norm_w': _L0_xattn_in['norm_w']}

def reference(x, ctx_1024, L0_xattn_wq, L0_xattn_wk, L0_xattn_wv, L0_xattn_wo, L0_xattn_norm_w):
    import jax
    import jax.numpy as jnp

    def _L0_xattn_ref(hidden_states, key_value_states, wq, wk, wv, wo, norm_w):
        import jax, jax.numpy as jnp
        import numpy as np
        B, Q, KV = (2, 512, 512)
        D_MODEL = 256
        N_HEADS = 16
        D_KV = 64
        EPS = 1e-06
        var = jnp.mean(jnp.square(hidden_states), axis=-1, keepdims=True)
        normed = hidden_states * jax.lax.rsqrt(var + EPS) * norm_w
        b, q_len, _ = hidden_states.shape
        kv_len = key_value_states.shape[1]

        def split_heads(x):
            return x.reshape(b, -1, N_HEADS, D_KV).transpose(0, 2, 1, 3)
        q = split_heads(normed @ wq)
        k = split_heads(key_value_states @ wk)
        v = split_heads(key_value_states @ wv)
        scores = jnp.einsum('bhqd,bhkd->bhqk', q, k)
        attn = jax.nn.softmax(scores.astype(jnp.float32), axis=-1).astype(scores.dtype)
        ctx = jnp.einsum('bhqk,bhkd->bhqd', attn, v)
        ctx = ctx.transpose(0, 2, 1, 3).reshape(b, q_len, N_HEADS * D_KV)
        attn_out = ctx @ wo
        return hidden_states + attn_out
    x = _L0_xattn_ref(x, ctx_1024, L0_xattn_wq, L0_xattn_wk, L0_xattn_wv, L0_xattn_wo, L0_xattn_norm_w)
    return x

_drawn_inputs = setup_inputs


def setup_inputs(seed=0):
    import zlib

    import numpy as np

    out = dict(_drawn_inputs(seed))
    spreads = {'L0_xattn_norm_w': (1.0, 0.6)}
    factors = {}
    for name, (base, spread) in spreads.items():
        noise = np.random.default_rng([zlib.crc32(name.encode()), seed]).standard_normal(out[name].shape)
        drawn = base * np.exp(spread * noise) if base else spread * noise
        out[name] = jnp.asarray(drawn.astype(out[name].dtype))
    for name, factor in factors.items():
        out[name] = (out[name] * factor).astype(out[name].dtype)
    return out
```

```python
import concourse.bass as bass
from concourse import mybir
from contextlib import ExitStack


def cross_attention_program(nc, x, ctx_in, wq, wk, wv, wo, norm_w, out):
    fp32 = mybir.dt.float32
    f32r = mybir.dt.float32r
    ALU = mybir.AluOpType
    ACT = mybir.ActivationFunctionType
    AX = mybir.AxisListType

    P = 128
    B, Q, D = x.shape
    KV = ctx_in.shape[1]
    INNER = wq.shape[1]
    DK = 64
    EPS = 1e-6
    NT = INNER // P
    NG = B * NT
    DC = D // P
    KT = KV // P
    QT = Q // P
    BANK = 512
    KH_ = KV // BANK
    NX = B * Q // P
    NC = B * KV // P
    NP = 4
    ROWS = 2 * QT
    NMAX = 2 * QT * KH_

    ctx = ExitStack()
    with ctx:
        def sb(name, shape, dt):
            return ctx.enter_context(nc.sbuf_tensor(name, shape, dt))

        def sem(name):
            return ctx.enter_context(nc.semaphore(name))

        cT = sb("cT", [P, 2, DC, B * KV], f32r)
        xT = sb("xT", [P, 2, DC, B * Q], f32r)
        wT = sb("w_split", [P, 2, 2, DC, P], f32r)
        kst = sb("k_stacks", [P, 2, 2, 2, KV], f32r)
        qst = sb("q_stacks", [P, 2, 2, 2, Q], f32r)
        khl = sb("k_split", [P, 2, KV], f32r)
        qhl = sb("q_split", [P, 2, Q], f32r)
        ctxT = sb("ctxT", [P, B, NT, Q], fp32)
        probs = sb("probs", [P, NP, 2, Q], fp32)
        vals = sb("vals", [P, 2, KT, P], fp32)
        wraw = sb("w_raw", [P, 2, DC, P], fp32)
        acc = sb("acc", [P, 2, Q], fp32)
        accp = sb("acc_pool", [P, 2, Q], fp32)
        rec = sb("rec", [P, Q], fp32)
        xres = sb("xres", [P, NX, D], fp32)
        wo_raw = sb("wo_raw", [P, NT, D], fp32)
        osb = sb("osb", [P, 4, D], fp32)
        mask = sb("mask", [ROWS, ROWS, P], fp32)
        ident = sb("ident", [P, P], fp32)
        ones = sb("ones", [P, DK], fp32)
        nw = sb("nw", [P, DC], fp32)
        ssq = sb("ssq", [P, NX], fp32)
        rstd = sb("rstd", [P, NX], fp32)
        half = sb("minus_half", [P, NX], fp32)
        mpart = sb("mpart", [P, 2 * QT, KH_], fp32)
        mcol = sb("mcol", [P, 2 * QT], fp32)
        v_dram = nc.dram_tensor("v_scratch", [B * KV, INNER], fp32, kind="Internal").ap()

        craw = ctxT[:, 0, :, :].rearrange("p a (b d) -> p (a b) d", d=D)
        xn = ctxT[:, 1, 0:NX * D // Q, :].rearrange("p a (b d) -> p (a b) d", d=D)
        wv_raw = probs[:, 0:2].rearrange("p s j q -> p s (j q)")
        stage = probs[:, 2:4].rearrange("p s j q -> p (s j) q")
        wv_hl = [kst[:, 1, i].rearrange("p j k -> p (j k)").rearrange("p (c n) -> p c n", c=DC)
                 for i in range(2)]
        wo_hl = xT[:].rearrange("p h c t -> p h (c t)").rearrange("p h (n d) -> p h n d", d=D)
        o0 = cT[:].rearrange("p h c t -> p h (c t)").rearrange("p h (n q) -> p h n q", q=Q)
        o1_hi = kst[:, 0].rearrange("p s j k -> p (s j k)").rearrange("p (n q) -> p n q", q=Q)
        o1_lo = [qst[:, 0].rearrange("p s j q -> p (s j) q"),
                 khl[:].rearrange("p h k -> p (h k)").rearrange("p (n q) -> p n q", q=Q)]

        def o_split(b, n):
            if b == 0:
                return o0[:, 0, n, :], o0[:, 1, n, :]
            return o1_hi[:, n, :], o1_lo[n // 4][:, n % 4, :]

        ps = ctx.enter_context(nc.psum_tensor("ps", [P, 8, BANK], fp32))
        S = [ps[:, 0:2, :], ps[:, 2:4, :]]
        PV = ps[:, 4, :]
        AUX = [ps[:, 5, :], ps[:, 6, :], ps[:, 7, :]]

        ld_x = sem("ld_x")
        ld_c = [sem(f"ld_c{i}") for i in range(4)]
        ld_nw = sem("ld_nw")
        ld_wv = sem("ld_wv")
        ld_wo = sem("ld_wo")
        ld_w = sem("ld_w")
        ld_v = [sem(f"ld_v{i}") for i in range(2)]
        st_v = [sem(f"st_v{i}") for i in range(4)]
        st_o = [sem(f"st_o{i}") for i in range(4)]
        const = sem("const")
        sq_done = sem("sq_done")
        ms_done = sem("ms_done")
        rstd_done = sem("rstd_done")
        xn_done = sem("xn_done")
        tr_ready = sem("tr_ready")
        tr_hi = sem("tr_hi")
        tr_lo = sem("tr_lo")
        wv_hi = sem("wv_hi")
        wv_lo = sem("wv_lo")
        w_hi = sem("w_hi")
        w_lo = sem("w_lo")
        v_ready = sem("v_ready")
        v_act = sem("v_act")
        v_dve = sem("v_dve")
        aux_ready = sem("aux_ready")
        aux_free = sem("aux_free")
        hi_done = sem("hi_done")
        st_k = sem("st_k")
        st_q = sem("st_q")
        mcol_ready = sem("mcol_ready")
        s_ready = sem("s_ready")
        p_ready = sem("p_ready")
        pv_done = sem("pv_done")
        ctx_evac = sem("ctx_evac")
        norm_done = sem("norm_done")
        add_dve = sem("add_dve")
        add_pool = sem("add_pool")
        wo_hi = sem("wo_hi")
        wo_lo = sem("wo_lo")
        o_hi = sem("o_hi")
        o_lo = sem("o_lo")
        o_res = sem("o_res")
        zeroed = sem("zeroed")
        rows_k = sem("rows_k")
        rows_q = sem("rows_q")

        PER = 3 + 1 + NMAX + 1

        def aux(g, what, i=0):
            early = isinstance(g, int) and g < 1
            den = 0 if early else 1
            a = {"k": i, "q": 2, "den": 3, "max": 3 + den + i, "maxT": 3 + den + NMAX}[what]
            if early:
                n = (PER - 1) * (g + 1) + a
                return AUX[n % 3], n
            n = 2 * (PER - 1) + a - PER
            return AUX[n % 3], PER * g + n

        TAIL = aux(NG - 1, "k")[1]

        def tail(i):
            return AUX[(TAIL + i) % 3], TAIL + i

        DEN_PREV, WO0, DEN_LAST, WO1 = 0, 1, 1 + QT, 2 + QT
        DENS_FREE = TAIL + 2

        def iterations(eng, body):
            body(0, 0, 0)
            body(1, 1, 0)
            with eng.Fori(1, NT - 1) as t:
                body(2 * t, 0, t)
                body(2 * t + 1, 1, t)
            body(NG - 2, 0, NT - 1)
            body(NG - 1, 1, NT - 1)

        def is_last(g):
            return isinstance(g, int) and g == NG - 1

        def is_first(g):
            return isinstance(g, int) and g == 0

        block = ctx.enter_context(nc.Block())

        def w_columns(w, t):
            return w.rearrange("(c p) (n m) -> p c n m", p=P, m=P)[:, :, t, :]

        @block.sync
        def _(sp):
            def load_w(t):
                sp.dma_start(wraw[:, 0], w_columns(wq, t)).then_inc(ld_w, 16)
                sp.dma_start(wraw[:, 1], w_columns(wk, t)).then_inc(ld_w, 16)

            x_rows = x.rearrange("b (n p) d -> p (b n) d", p=P)
            c_rows = ctx_in.rearrange("b (n p) d -> p (b n) d", p=P)
            sp.dma_start(xres[:], x_rows).then_inc(ld_x, 16)
            for i in range(4):
                sp.dma_start(craw[:, 4 * i:4 * i + 4], c_rows[:, 4 * i:4 * i + 4]).then_inc(ld_c[i], 16)
            with nc.allow_non_contiguous_dma(reason="256 scales, one per partition and chunk"):
                sp.dma_start(nw[:], norm_w.rearrange("(c p) -> p c", p=P)).then_inc(ld_nw, 16)
            load_w(0)
            sp.dma_start(wv_raw, wv.rearrange("(c p) n -> p c n", p=P)).then_inc(ld_wv, 16)
            sp.dma_start(wo_raw[:], wo.rearrange("(n p) d -> p n d", p=P)).then_inc(ld_wo, 16)

            def stacks(g, r, what):
                if what == "k":
                    sp.wait_ge(aux_free, aux(g, "k", 1)[1] + 1)
                    dst, src, done = kst, khl, st_k
                    plan = [(0, 0, 0), (0, DK, 1), (1, 0, 0)]
                else:
                    sp.wait_ge(aux_free, aux(g, "q")[1] + 1)
                    dst, src, done = qst, qhl, st_q
                    plan = [(0, 0, 0), (0, DK, 0), (1, 0, 1)]
                for j in range(2):
                    for s, row, h in plan:
                        sp.dma_start(dst[row:row + DK, r, s, j].bitcast(fp32),
                                     src[DK * j:DK * j + DK, h].bitcast(fp32)).then_inc(done, 16)

            def load_v(g, r, t):
                src = v_dram.rearrange("(b k p) (n m) -> p b k n m", p=P, k=KT, m=P)[:, r, :, t, :]
                sp.dma_start(vals[:, r], src).then_inc(ld_v[r], 16)

            stacks(-1, 0, "k")
            stacks(-1, 0, "q")
            v_rows = v_dram.rearrange("(n p) (h c) -> p n h c", p=P, c=BANK)
            for v in range(2 * NC):
                sp.wait_ge(v_act if v % 2 == 0 else v_dve, v // 2 + 1)
                sp.dma_start(v_rows[:, v % NC, v // NC], stage[:, v % 4]).then_inc(st_v[v % 4], 16)
            for i in range(4):
                sp.wait_ge(st_v[i], 16 * (2 * NC // 4))
            load_v(0, 0, 0)

            def body(g, r, t):
                o = 1 - r
                if not is_last(g):
                    if not is_first(g):
                        sp.wait_ge(pv_done, KT * g)
                    load_v(g + 1, o, t + r)
                    if r == 0 and not (isinstance(t, int) and t == NT - 1):
                        sp.wait_ge(w_lo, t + 1)
                        load_w(t + 1)
                    if is_first(g):
                        sp.wait_ge(v_ready, 2 * NC)
                    else:
                        sp.wait_ge(s_ready, KT * g)
                    stacks(g, o, "k")
                    stacks(g, o, "q")

            iterations(sp, body)
            o_rows = out.rearrange("b (n p) d -> p (b n) d", p=P)
            for n in range(NX):
                sp.wait_ge(o_res, n + 1)
                sp.dma_start(o_rows[:, n], osb[:, n % 4]).then_inc(st_o[n % 4], 16)
            for i in range(4):
                sp.wait_ge(st_o[i], 16 * (NX // 4))

        @block.gpsimd
        def _(pool):
            nc.gpsimd.memset(ident[:], 0.0).then_inc(zeroed, 1)
            nc.gpsimd.memset(mask[:], 0.0).then_inc(zeroed, 1)
            pool.wait_ge(zeroed, 2)
            nc.gpsimd.affine_select(out=ident[:], in_=ident[:], compare_op=ALU.not_equal, fill=1.0, base=0,
                                    pattern=[[-1, P]], channel_multiplier=1).then_inc(const, 1)
            nc.gpsimd.affine_select(out=mask[:], in_=mask[:], compare_op=ALU.not_equal, fill=1.0, base=0,
                                    pattern=[[-1, ROWS], [0, P]], channel_multiplier=1).then_inc(const, 1)
            nc.gpsimd.memset(ones[:], 1.0).then_inc(const, 1)
            nc.gpsimd.memset(half[:], -0.5).then_inc(const, 1)
            pool.wait_ge(sq_done, NX)
            nc.gpsimd.tensor_scalar(rstd[:], ssq[:], 1.0 / D, EPS, ALU.mult, ALU.add).then_inc(ms_done, 1)
            pool.wait_ge(ms_done, 1)
            pool.wait_ge(const, 4)
            nc.gpsimd.tensor_tensor(rstd[:], rstd[:], half[:], ALU.pow).then_inc(rstd_done, 1)

            def body(g, r, t):
                pool.wait_ge(p_ready, KT * g + 2)
                if not is_first(g):
                    pool.wait_ge(add_dve, 4 * g)
                nc.gpsimd.tensor_tensor(accp[:], probs[:, 0], probs[:, 1], ALU.add).then_inc(add_pool, 1)
                for s in (2, 3):
                    pool.wait_ge(p_ready, KT * g + s + 1)
                    pool.wait_ge(add_pool, 3 * g + s - 1)
                    nc.gpsimd.tensor_tensor(accp[:], accp[:], probs[:, s], ALU.add).then_inc(add_pool, 1)

            iterations(pool, body)

        @block.scalar
        def _(act):
            act.wait_ge(ld_x, 16)
            for n in range(NX):
                nc.scalar.activation(xn[:, n], xres[:, n], ACT.Square,
                                     accum_out=ssq[:, n:n + 1]).then_inc(sq_done, 1)
            act.wait_ge(ld_wv, 16)
            nc.scalar.copy(wv_hl[0], wv_raw).then_inc(wv_hi, 1)

            def split_w_hi(t):
                act.wait_ge(ld_w, 32 * (t + 1))
                nc.scalar.copy(wT[:, 0], wraw[:]).then_inc(w_hi, 1)

            split_w_hi(0)
            for u in range(2 * NC // 4):
                grp, c = u // DC, u % DC
                act.wait_ge(tr_ready, u + 1)
                nc.scalar.copy(cT[:, 0, c, BANK * grp:BANK * grp + BANK], ps[:, u % 4, :]).then_inc(tr_hi, 1)
            act.wait_ge(ld_nw, 16)
            for u in range(2 * NX // 4):
                grp, c = u // DC, u % DC
                n = u + 2 * NC // 4
                act.wait_ge(tr_ready, n + 1)
                nc.scalar.activation(xT[:, 0, c, BANK * grp:BANK * grp + BANK], ps[:, n % 4, :], ACT.Copy,
                                     scale=nw[:, c:c + 1]).then_inc(tr_hi, 1)

            def hi(g, what, i, n):
                bank, u = aux(g, what, i)
                act.wait_ge(aux_ready, u + 1)
                dst = khl[:, 0, BANK * i:BANK * i + BANK] if what == "k" else qhl[:, 0, :]
                if not (isinstance(g, int) and g == -1):
                    act.wait_ge(st_k if what == "k" else st_q, 96 * (g + 1))
                nc.scalar.copy(dst, bank).then_inc(hi_done, 1)

            for what, i in (("k", 0), ("k", 1), ("q", 0)):
                hi(-1, what, i, 0)
            for v in range(0, 2 * NC, 2):
                act.wait_ge(v_ready, v + 1)
                if v >= 4:
                    act.wait_ge(st_v[v % 4], 16 * (v // 4))
                nc.scalar.copy(stage[:, v % 4], ps[:, v % 4, :]).then_inc(v_act, 1)

            for i in range(4):
                act.wait_ge(st_v[i], 16 * (2 * NC // 4))

            def exp(g, s):
                act.wait_ge(s_ready, KT * g + s + 1)
                first = is_first(g)
                if s >= 4 or not first:
                    act.wait_ge(pv_done, KT * g + s - 3)
                if s >= 4:
                    act.wait_ge(add_pool, 3 * g + max(1, s - 4))
                elif not first:
                    act.wait_ge(add_dve, 4 * g - 4 + max(1, s))
                nc.scalar.activation(probs[:, s % NP], S[s % 2], ACT.Exp).then_inc(p_ready, 1)

            def evacuate(g, r, t):
                act.wait_ge(pv_done, KT * g)
                nc.scalar.copy(ctxT[:, 1 - r, t + r - 1, :], PV).then_inc(ctx_evac, 1)

            def body(g, r, t):
                last = is_last(g)
                for s in range(KT):
                    exp(g, s)
                    if s == 0:
                        if not is_first(g):
                            evacuate(g, r, t)
                        if not last:
                            hi(g, "k", 0, 0)
                            hi(g, "k", 1, 0)
                        else:
                            act.wait_ge(ld_wo, 16)
                            nc.scalar.copy(wo_hl[:, 0], wo_raw[:]).then_inc(wo_hi, 1)
                    if s == 1 and not last:
                        hi(g, "q", 0, 0)
                    if s == 2 and r == 0 and not (isinstance(t, int) and t == NT - 1):
                        split_w_hi(t + 1)
                    if s >= 3 and last:
                        for n in range((s - 3) * NT // 5, (s - 2) * NT // 5):
                            o_hi_split(0, n)

            def o_hi_split(b, n):
                act.wait_ge(norm_done, 2 * n + b + 1)
                nc.scalar.copy(o_split(b, n)[0], ctxT[:, b, n, :]).then_inc(o_hi, 1)

            iterations(act, body)
            for n in range(NT - 1):
                o_hi_split(1, n)
            evacuate(NG, 0, NT)
            o_hi_split(1, NT - 1)

        @block.vector
        def _(dve):
            def const_rows(r):
                nc.vector.memset(kst[DK:P, r, 1].bitcast(fp32), 0.0).then_inc(rows_k, 1)
                dve.wait_ge(rows_k, 1 + 2 * r)
                nc.vector.memset(kst[DK:DK + ROWS, r, 1].bitcast(fp32), -1.0).then_inc(rows_k, 1)

            const_rows(0)
            nc.vector.memset(qst[DK:P, :, 1].bitcast(fp32), 0.0).then_inc(rows_q, 1)
            dve.wait_ge(rstd_done, 1)
            for n in range(NX):
                nc.vector.tensor_scalar(xn[:, n], xres[:, n], rstd[:, n:n + 1], None, ALU.mult).then_inc(xn_done, 1)
            dve.wait_ge(wv_hi, 1)
            nc.vector.tensor_tensor(wv_hl[1], wv_raw, wv_hl[0].bitcast(fp32), ALU.subtract).then_inc(wv_lo, 1)

            def split_w_lo(t):
                dve.wait_ge(w_hi, t + 1)
                nc.vector.tensor_tensor(wT[:, 1], wraw[:], wT[:, 0].bitcast(fp32), ALU.subtract).then_inc(w_lo, 1)

            split_w_lo(0)
            for u in range(2 * NC // 4):
                grp, c = u // DC, u % DC
                cols = slice(BANK * grp, BANK * grp + BANK)
                dve.wait_ge(tr_hi, u + 1)
                nc.vector.tensor_tensor(cT[:, 1, c, cols], ps[:, u % 4, :], cT[:, 0, c, cols].bitcast(fp32),
                                        ALU.subtract).then_inc(tr_lo, 1)
            for u in range(2 * NX // 4):
                grp, c = u // DC, u % DC
                n = u + 2 * NC // 4
                cols = slice(BANK * grp, BANK * grp + BANK)
                dve.wait_ge(tr_hi, n + 1)
                nc.vector.scalar_tensor_tensor(out=xT[:, 1, c, cols], in0=ps[:, n % 4, :], scalar=nw[:, c:c + 1],
                                               in1=xT[:, 0, c, cols].bitcast(fp32), op0=ALU.mult,
                                               op1=ALU.subtract).then_inc(tr_lo, 1)

            def lo(g, what, i, n):
                bank, u = aux(g, what, i)
                t = khl if what == "k" else qhl
                cols = slice(BANK * i, BANK * i + BANK)
                dve.wait_ge(hi_done, 3 * (g + 1) + n + 1)
                nc.vector.tensor_tensor(t[:, 1, cols], bank, t[:, 0, cols].bitcast(fp32),
                                        ALU.subtract).then_inc(aux_free, 1)

            def lows(g):
                lo(g, "k", 0, 0)
                lo(g, "k", 1, 1)
                lo(g, "q", 0, 2)

            def reduce(g, i):
                bank, u = aux(g, "max", i)
                dve.wait_ge(aux_ready, u + 1)
                nc.vector.reduce_max(mpart[:, i // KH_, i % KH_:i % KH_ + 1], bank, AX.X).then_inc(aux_free, 1)

            def combine(g):
                dve.wait_ge(aux_free, aux(g, "max", NMAX - 1)[1] + 1)
                nc.vector.reduce_max(mcol[:], mpart[:], AX.X).then_inc(mcol_ready, 1)

            def spread(g, r):
                bank, u = aux(g, "maxT")
                dve.wait_ge(aux_ready, u + 1)
                dst = qst[DK:DK + ROWS, r, 1].rearrange("p j (n q) -> p (j n) q", q=P)
                src = bank[0:ROWS, 0:P].unsqueeze(1).to_broadcast([ROWS, ROWS, P])
                nc.vector.tensor_tensor(dst, src, mask[:], ALU.mult).then_inc(aux_free, 1)

            lows(-1)
            i = 0
            for v in range(2 * NC):
                if v >= NC and i < NMAX:
                    reduce(-1, i)
                    i += 1
                if v % 2 == 1:
                    dve.wait_ge(v_ready, v + 1)
                    if v >= 4:
                        dve.wait_ge(st_v[v % 4], 16 * (v // 4))
                    nc.vector.tensor_copy(stage[:, v % 4], ps[:, v % 4, :]).then_inc(v_dve, 1)
            combine(-1)
            dve.wait_ge(const, 4)
            dve.wait_ge(rows_q, 1)
            spread(-1, 0)
            const_rows(1)

            def add(g, k):
                if k == 0:
                    dve.wait_ge(p_ready, KT * g + 6)
                    ins = probs[:, 0], probs[:, 1]
                elif k < 3:
                    dve.wait_ge(p_ready, KT * g + 6 + k)
                    dve.wait_ge(add_dve, 4 * g + k)
                    ins = acc[:], probs[:, 1 + k]
                else:
                    dve.wait_ge(add_pool, 3 * g + 3)
                    dve.wait_ge(add_dve, 4 * g + k)
                    ins = acc[:], accp[:]
                nc.vector.tensor_tensor(acc[:], ins[0], ins[1], ALU.add).then_inc(add_dve, 1)

            def normalise(g, unit, b, n):
                bank, u = unit
                dve.wait_ge(aux_ready, u + 1)
                nc.vector.reciprocal(rec[:], bank).then_inc(aux_free, 1)
                dve.wait_ge(ctx_evac, g)
                dve.wait_ge(aux_free, DENS_FREE if isinstance(g, int) and g == NG else u + 1)
                nc.vector.tensor_tensor(ctxT[:, b, n, :], ctxT[:, b, n, :], rec[:], ALU.mult).then_inc(norm_done, 1)

            def o_lo_split(b, n):
                dve.wait_ge(o_hi, b * NT + n + 1)
                h, l = o_split(b, n)
                nc.vector.tensor_tensor(l, ctxT[:, b, n, :], h.bitcast(fp32), ALU.subtract).then_inc(o_lo, 1)

            def residual(n, unit):
                bank, u = unit
                dve.wait_ge(aux_ready, u + 1)
                if n >= 4:
                    dve.wait_ge(st_o[n % 4], 16 * (n // 4))
                nc.vector.tensor_tensor(osb[:, n % 4], bank[:, 0:D], xres[:, n], ALU.add).then_inc(o_res, 1)

            def body(g, r, t):
                last = is_last(g)
                if not is_first(g):
                    add(g - 1, 2)
                    add(g - 1, 3)
                if not last:
                    lows(g)
                if not is_first(g):
                    normalise(g, tail(DEN_PREV) if last else aux(g, "den"), 1 - r, t + r - 1)
                if r == 0 and not (isinstance(t, int) and t == NT - 1):
                    split_w_lo(t + 1)
                if last:
                    dve.wait_ge(wo_hi, 1)
                    nc.vector.tensor_tensor(wo_hl[:, 1], wo_raw[:], wo_hl[:, 0].bitcast(fp32),
                                            ALU.subtract).then_inc(wo_lo, 1)
                    for n in range(NT // 2):
                        o_lo_split(0, n)
                    add(g, 0)
                    for n in range(NT // 2, NT):
                        o_lo_split(0, n)
                    add(g, 1)
                else:
                    for i in range(NMAX - 4):
                        reduce(g, i)
                    reduce(g, NMAX - 4)
                    reduce(g, NMAX - 3)
                    add(g, 0)
                    reduce(g, NMAX - 2)
                    reduce(g, NMAX - 1)
                    combine(g)
                    add(g, 1)
                    if not is_first(g):
                        pass
                    spread(g, 1 - r)

            iterations(dve, body)
            add(NG - 1, 2)
            add(NG - 1, 3)
            for n in range(QT):
                residual(n, tail(WO0 + n))
                if n == 0:
                    pass
            for n in range(NT - 1):
                o_lo_split(1, n)
            normalise(NG, tail(DEN_LAST), 1, NT - 1)
            o_lo_split(1, NT - 1)
            for n in range(QT):
                residual(QT + n, tail(WO1 + n))

        @block.tensor
        def _(pe):
            mm = nc.tensor.matmul

            pe.wait_ge(const, 1)
            for u in range(2 * (NC + NX) // 4):
                if u < 2 * NC // 4:
                    src, grp, c = craw, u // DC, u % DC
                    pe.wait_ge(ld_c[grp], 16)
                else:
                    src, grp, c = xn, (u - 2 * NC // 4) // DC, u % DC
                    pe.wait_ge(xn_done, NX)
                if u >= 4:
                    pe.wait_ge(tr_lo, u - 3)
                for i in range(4):
                    last = nc.tensor.transpose(ps[:, u % 4, P * i:P * i + P],
                                               src[:, 4 * grp + i, P * c:P * c + P], ident[:])
                last.then_inc(tr_ready, 1)
            pe.wait_ge(tr_lo, 2 * (NC + NX) // 4)

            def aux_wait(u):
                if not (isinstance(u, int) and u < 3):
                    pe.wait_ge(aux_free, u - 2)

            def split_product(bank, lhs, rhs, chunks):
                terms = [(h, l, c) for c in range(chunks) for h, l in ((0, 0), (0, 1), (1, 0))]
                for i, (h, l, c) in enumerate(terms):
                    last = mm(bank, lhs(h, c), rhs(l, c), start=(i == 0), stop=(i == len(terms) - 1))
                return last

            def project(g, what, i, b):
                bank, u = aux(g, what, i)
                aux_wait(u)
                m = 1 if what == "k" else 0
                src, col = (cT, KV * b + BANK * i) if what == "k" else (xT, Q * b)
                split_product(bank, lambda h, c: wT[:, h, m, c], lambda h, c: src[:, h, c, col:col + BANK],
                              DC).then_inc(aux_ready, 1)

            def approx_scores(g, r, i):
                bank, u = aux(g, "max", i)
                j, q, k = i // (QT * KH_), i // KH_ % QT, i % KH_
                aux_wait(u)
                mm(bank, qst[:, r, 0, j, P * q:P * q + P], kst[:, r, 0, j, BANK * k:BANK * k + BANK],
                   start=True, stop=True).then_inc(aux_ready, 1)

            def max_rows(g):
                bank, u = aux(g, "maxT")
                pe.wait_ge(mcol_ready, g + 2)
                aux_wait(u)
                nc.tensor.transpose(bank[0:ROWS, 0:P], mcol[:], ident[:]).then_inc(aux_ready, 1)

            def scores(g, r, s):
                buf = S[s % 2]
                if not (is_first(g) and s < 2):
                    pe.wait_ge(p_ready, KT * g + s - 1)
                keys = slice(P * s, P * s + P)
                for j in range(2):
                    mm(buf[:, j], kst[:, r, 0, j, keys], qst[:, r, 0, j], start=True, stop=False)
                if s == 0:
                    pe.wait_ge(aux_free, aux(g - 1, "maxT")[1] + 1)
                    if is_first(g):
                        pe.wait_ge(rows_k, 2)
                    if isinstance(g, int) and g == 1:
                        pe.wait_ge(rows_k, 4)
                for j in range(2):
                    last = mm(buf[:, j], kst[:, r, 1, j, keys], qst[:, r, 1, j], start=False, stop=True)
                last.then_inc(s_ready, 1)

            def values(g, r, s, t):
                pe.wait_ge(p_ready, KT * g + s + 1)
                if s == 0:
                    pe.wait_ge(ld_v[r], 16 * (t + 1))
                    if not is_first(g):
                        pe.wait_ge(ctx_evac, g)
                for j in range(2):
                    rows = slice(DK * j, DK * j + DK)
                    last = mm(PV[rows, :], vals[:, r, s, rows], probs[:, s % NP, j],
                              start=(s == 0), stop=(s == KT - 1))
                last.then_inc(pv_done, 1)

            def denominators(g, unit):
                bank, u = unit
                pe.wait_ge(add_dve, 4 * g)
                if isinstance(g, int) and g == NG:
                    tail_wait(DEN_LAST)
                else:
                    aux_wait(u)
                for j in range(2):
                    last = mm(bank[DK * j:DK * j + DK, :], ones[:], acc[:, j], start=True, stop=True)
                last.then_inc(aux_ready, 1)

            def tail_wait(i):
                if i - 3 <= DEN_PREV:
                    pe.wait_ge(aux_free, TAIL + i - 2)
                elif i - 3 == DEN_LAST:
                    pe.wait_ge(aux_free, DENS_FREE)
                else:
                    pe.wait_ge(o_res, i - 3 - WO0 + 1 - (i - 3 > DEN_LAST))

            def output(b, n, i):
                bank, _ = tail(i)
                tail_wait(i)
                rows = slice(P * n, P * n + P)
                split_product(bank[:, 0:D], lambda h, c: o_split(b, c)[h][:, rows], lambda l, c: wo_hl[:, l, c],
                              NT).then_inc(aux_ready, 1)

            pe.wait_ge(w_lo, 1)
            for what, i in (("k", 0), ("k", 1), ("q", 0)):
                project(-1, what, i, 0)
            pe.wait_ge(wv_lo, 1)
            i = 0
            for v in range(2 * NC):
                if v >= 4:
                    pe.wait_ge(v_act if v % 2 == 0 else v_dve, (v - 4) // 2 + 1)
                rows = slice(P * (v % NC), P * (v % NC) + P)
                cols = slice(BANK * (v // NC), BANK * (v // NC) + BANK)
                split_product(ps[:, v % 4, :], lambda h, c: cT[:, h, c, rows], lambda l, c: wv_hl[l][:, c, cols],
                              DC).then_inc(v_ready, 1)
                if v >= NC and i < NMAX:
                    if i == 0:
                        pe.wait_ge(st_k, 96)
                        pe.wait_ge(st_q, 96)
                    approx_scores(-1, 0, i)
                    i += 1
            max_rows(-1)
            pe.wait_ge(v_act, NC)
            pe.wait_ge(v_dve, NC)

            def body(g, r, t):
                last = is_last(g)
                for s in range(KT):
                    scores(g, r, s)
                    if s > 0:
                        values(g, r, s - 1, t)
                    elif not is_first(g):
                        values(g - 1, 1 - r, KT - 1, t + r - 1)
                    if s == 0 and not last:
                        pe.wait_ge(w_lo, t + r + 1)
                        project(g, "k", 0, 1 - r)
                        project(g, "k", 1, 1 - r)
                    if s == 1 and not last:
                        project(g, "q", 0, 1 - r)
                    if s == 2 and not is_first(g):
                        denominators(g, tail(DEN_PREV) if last else aux(g, "den"))
                    if 3 <= s <= 6 and not last:
                        if s == 3:
                            pe.wait_ge(st_k, 96 * (g + 2))
                            pe.wait_ge(st_q, 96 * (g + 2))
                        for i in range((s - 3) * NMAX // 4, (s - 2) * NMAX // 4):
                            approx_scores(g, 1 - r, i)
                    if s == 7 and not last:
                        max_rows(g)

            iterations(pe, body)
            values(NG - 1, 1, KT - 1, NT - 1)
            pe.wait_ge(wo_lo, 1)
            pe.wait_ge(o_lo, NT)
            for n in range(QT):
                output(0, n, WO0 + n)
            denominators(NG, tail(DEN_LAST))
            pe.wait_ge(o_lo, 2 * NT)
            for n in range(QT):
                output(1, n, WO1 + n)


_INS = ['x', 'ctx_1024', 'L0_xattn_wq', 'L0_xattn_wk', 'L0_xattn_wv', 'L0_xattn_wo', 'L0_xattn_norm_w']


def kernel(**inputs):
    import numpy as _np
    import concourse.bacc as _bacc
    from concourse import mybir as _mybir
    from concourse.bass_utils import run_bass_kernel_spmd as _run

    nc = _bacc.Bacc("TRN2", target_bir_lowering=False, num_devices=1)
    arrays, args = {}, []
    for name in _INS:
        a = _np.ascontiguousarray(inputs[name])
        arrays[f"in_{name}"] = a
        args.append(nc.dram_tensor(f"in_{name}", a.shape, _mybir.dt.from_np(a.dtype), kind="ExternalInput").ap())
    args.append(nc.dram_tensor("out_0", tuple(inputs['x'].shape), _mybir.dt.float32, kind="ExternalOutput").ap())
    cross_attention_program(nc, *args)
    r = _run(nc, [arrays], core_ids=[0])
    return r.results[0]["out_0"]
```

```python
import concourse.bass as bass
from concourse import mybir
from contextlib import ExitStack


def cross_attention_program(nc, x, ctx_in, wq, wk, wv, wo, norm_w, out):
    fp32 = mybir.dt.float32
    f32r = mybir.dt.float32r
    ALU = mybir.AluOpType
    ACT = mybir.ActivationFunctionType
    AX = mybir.AxisListType

    P = 128
    B, Q, D = x.shape
    KV = ctx_in.shape[1]
    INNER = wq.shape[1]
    DK = 64
    EPS = 1e-6
    NT = INNER // P
    NG = B * NT
    DC = D // P
    KT = KV // P
    QT = Q // P
    BANK = 512
    KH_ = KV // BANK
    NX = B * Q // P
    NC = B * KV // P
    NP = 4
    ROWS = 2 * QT
    NMAX = 2 * QT * KH_

    ctx = ExitStack()
    with ctx:
        def sb(name, shape, dt):
            return ctx.enter_context(nc.sbuf_tensor(name, shape, dt))

        def sem(name):
            return ctx.enter_context(nc.semaphore(name))

        cT = sb("cT", [P, 2, DC, B * KV], f32r)
        xT = sb("xT", [P, 2, DC, B * Q], f32r)
        wT = sb("w_split", [P, 2, 2, DC, P], f32r)
        kst = sb("k_stacks", [P, 2, 2, 2, KV], f32r)
        qst = sb("q_stacks", [P, 2, 2, 2, Q], f32r)
        khl = sb("k_split", [P, 2, KV], f32r)
        qhl = sb("q_split", [P, 2, Q], f32r)
        ctxT = sb("ctxT", [P, B, NT, Q], fp32)
        probs = sb("probs", [P, NP, 2, Q], fp32)
        vals = sb("vals", [P, 2, KT, P], fp32)
        wraw = sb("w_raw", [P, 2, DC, P], fp32)
        acc = sb("acc", [P, 2, Q], fp32)
        accp = sb("acc_pool", [P, 2, Q], fp32)
        rec = sb("rec", [P, Q], fp32)
        xres = sb("xres", [P, NX, D], fp32)
        wo_raw = sb("wo_raw", [P, NT, D], fp32)
        osb = sb("osb", [P, 4, D], fp32)
        mask = sb("mask", [ROWS, ROWS, P], fp32)
        ident = sb("ident", [P, P], fp32)
        ones = sb("ones", [P, DK], fp32)
        nw = sb("nw", [P, DC], fp32)
        ssq = sb("ssq", [P, NX], fp32)
        rstd = sb("rstd", [P, NX], fp32)
        half = sb("minus_half", [P, NX], fp32)
        mpart = sb("mpart", [P, 2 * QT, KH_], fp32)
        mcol = sb("mcol", [P, 2 * QT], fp32)
        v_dram = nc.dram_tensor("v_scratch", [B * KV, INNER], fp32, kind="Internal").ap()

        craw = ctxT[:, 0, :, :].rearrange("p a (b d) -> p (a b) d", d=D)
        xn = ctxT[:, 1, 0:NX * D // Q, :].rearrange("p a (b d) -> p (a b) d", d=D)
        wv_raw = probs[:, 0:2].rearrange("p s j q -> p s (j q)")
        stage = probs[:, 2:4].rearrange("p s j q -> p (s j) q")
        wv_hl = [kst[:, 1, i].rearrange("p j k -> p (j k)").rearrange("p (c n) -> p c n", c=DC)
                 for i in range(2)]
        wo_hl = xT[:].rearrange("p h c t -> p h (c t)").rearrange("p h (n d) -> p h n d", d=D)
        o0 = cT[:].rearrange("p h c t -> p h (c t)").rearrange("p h (n q) -> p h n q", q=Q)
        o1_hi = kst[:, 0].rearrange("p s j k -> p (s j k)").rearrange("p (n q) -> p n q", q=Q)
        o1_lo = [qst[:, 0].rearrange("p s j q -> p (s j) q"),
                 khl[:].rearrange("p h k -> p (h k)").rearrange("p (n q) -> p n q", q=Q)]

        def o_split(b, n):
            if b == 0:
                return o0[:, 0, n, :], o0[:, 1, n, :]
            return o1_hi[:, n, :], o1_lo[n // 4][:, n % 4, :]

        ps = ctx.enter_context(nc.psum_tensor("ps", [P, 8, BANK], fp32))
        S = [ps[:, 0:2, :], ps[:, 2:4, :]]
        PV = ps[:, 4, :]
        AUX = [ps[:, 5, :], ps[:, 6, :], ps[:, 7, :]]

        ld_x = sem("ld_x")
        ld_c = [sem(f"ld_c{i}") for i in range(4)]
        ld_nw = sem("ld_nw")
        ld_wv = sem("ld_wv")
        ld_wo = sem("ld_wo")
        ld_w = sem("ld_w")
        ld_v = [sem(f"ld_v{i}") for i in range(2)]
        st_v = [sem(f"st_v{i}") for i in range(4)]
        st_o = [sem(f"st_o{i}") for i in range(4)]
        const = sem("const")
        sq_done = sem("sq_done")
        ms_done = sem("ms_done")
        rstd_done = sem("rstd_done")
        xn_done = sem("xn_done")
        tr_ready = sem("tr_ready")
        tr_hi = sem("tr_hi")
        tr_lo = sem("tr_lo")
        wv_hi = sem("wv_hi")
        wv_lo = sem("wv_lo")
        w_hi = sem("w_hi")
        w_lo = sem("w_lo")
        v_ready = sem("v_ready")
        v_act = sem("v_act")
        v_dve = sem("v_dve")
        aux_ready = sem("aux_ready")
        aux_free = sem("aux_free")
        hi_done = sem("hi_done")
        st_j = [sem(f"st_j{j}") for j in range(2)]
        st_2 = sem("st_2")
        mcol_ready = sem("mcol_ready")
        s_ready = sem("s_ready")
        p_ready = sem("p_ready")
        pv_done = sem("pv_done")
        ctx_evac = sem("ctx_evac")
        norm_done = sem("norm_done")
        add_dve = sem("add_dve")
        add_pool = sem("add_pool")
        wo_hi = sem("wo_hi")
        wo_lo = sem("wo_lo")
        o_hi = sem("o_hi")
        o_lo = sem("o_lo")
        o_res = sem("o_res")
        zeroed = sem("zeroed")
        rows_k = sem("rows_k")
        rows_q = sem("rows_q")

        PLAN = [[],
                [("max", i) for i in range(0, 4)],
                [("max", i) for i in range(4, 7)] + [("den", 0)],
                [("k", 0), ("k", 1)],
                [("max", i) for i in range(7, 11)],
                [("max", i) for i in range(11, 16)],
                [("q", 0), ("maxT", 0)],
                []]
        PROJECTIONS = [("k", 0), ("k", 1), ("q", 0)]
        UNITS = [u for units in PLAN for u in units]
        PER = len(UNITS)

        def has(g, what):
            if not isinstance(g, int):
                return True
            return {"den": g >= 1, "k": g < NG - 2, "q": g < NG - 2, "max": g < NG - 1, "maxT": g < NG - 1}[what]

        def order(g):
            if g == -2:
                return PROJECTIONS
            if g == -1:
                return [("max", i) for i in range(NMAX)] + [("maxT", 0)] + PROJECTIONS
            return [u for u in UNITS if has(g, u[0])]

        def before(g):
            return sum(len(order(h)) for h in range(-2, g))

        def aux(g, what, i=0):
            if isinstance(g, int):
                n = before(g) + order(g).index((what, i))
                return AUX[n % 3], n
            n = before(2) - 2 * PER + UNITS.index((what, i))
            return AUX[n % 3], PER * g + n

        TAIL = before(NG - 1)

        def tail(i):
            return AUX[(TAIL + i) % 3], TAIL + i

        DEN_PREV, WO0, DEN_LAST, WO1 = 0, 1, 1 + QT, 2 + QT
        DENS_FREE = TAIL + 2

        def iterations(eng, body):
            body(0, 0, 0)
            body(1, 1, 0)
            with eng.Fori(1, NT - 2) as t:
                body(2 * t, 0, t)
                body(2 * t + 1, 1, t)
            body(NG - 4, 0, NT - 2)
            body(NG - 3, 1, NT - 2)
            body(NG - 2, 0, NT - 1)
            body(NG - 1, 1, NT - 1)

        def more_weights(t):
            return not isinstance(t, int) or t + 2 < NT

        def is_last(g):
            return isinstance(g, int) and g == NG - 1

        def is_first(g):
            return isinstance(g, int) and g == 0

        POOLED = 5
        POOL_ADDS = POOLED - 1
        DVE_ADDS = KT - POOLED
        STACKED = 4 * 16
        STACKED2 = 2 * 16

        block = ctx.enter_context(nc.Block())

        def w_columns(w, t):
            return w.rearrange("(c p) (n m) -> p c n m", p=P, m=P)[:, :, t, :]

        @block.sync
        def _(sp):
            def load_w(t):
                sp.dma_start(wraw[:, 0], w_columns(wq, t)).then_inc(ld_w, 16)
                sp.dma_start(wraw[:, 1], w_columns(wk, t)).then_inc(ld_w, 16)

            x_rows = x.rearrange("b (n p) d -> p (b n) d", p=P)
            c_rows = ctx_in.rearrange("b (n p) d -> p (b n) d", p=P)
            sp.dma_start(xres[:], x_rows).then_inc(ld_x, 16)
            for i in range(4):
                sp.dma_start(craw[:, 4 * i:4 * i + 4], c_rows[:, 4 * i:4 * i + 4]).then_inc(ld_c[i], 16)
            with nc.allow_non_contiguous_dma(reason="256 scales, one per partition and chunk"):
                sp.dma_start(nw[:], norm_w.rearrange("(c p) -> p c", p=P)).then_inc(ld_nw, 16)
            load_w(0)
            sp.dma_start(wv_raw, wv.rearrange("(c p) n -> p c n", p=P)).then_inc(ld_wv, 16)
            sp.dma_start(wo_raw[:], wo.rearrange("(n p) d -> p n d", p=P)).then_inc(ld_wo, 16)

            def stacks(g, r):
                def copy(dst, src, done):
                    sp.dma_start(dst.bitcast(fp32), src.bitcast(fp32)).then_inc(done, 16)

                sp.wait_ge(aux_free, aux(g, "k", 1)[1] + 1)
                for j in range(2):
                    rows = slice(DK * j, DK * j + DK)
                    copy(kst[0:DK, r, 0, j], khl[rows, 0], st_j[j])
                    copy(kst[DK:P, r, 0, j], khl[rows, 1], st_j[j])
                    if j == 0:
                        sp.wait_ge(aux_free, aux(g, "q")[1] + 1)
                    copy(qst[0:DK, r, :, j], qhl[rows], st_j[j])
                    copy(qst[DK:P, r, 0, j], qhl[rows, 0], st_j[j])
                for j in range(2):
                    copy(kst[0:DK, r, 1, j], khl[DK * j:DK * j + DK, 0], st_2)

            def load_v(g, r, t):
                src = v_dram.rearrange("(b k p) (n m) -> p b k n m", p=P, k=KT, m=P)[:, r, :, t, :]
                sp.dma_start(vals[:, r], src).then_inc(ld_v[r], 16)

            stacks(-2, 0)
            sp.wait_ge(w_lo, 1)
            load_w(1)
            v_rows = v_dram.rearrange("(n p) (h c) -> p n h c", p=P, c=BANK)
            for v in range(2 * NC):
                sp.wait_ge(v_act if v % 2 == 0 else v_dve, v // 2 + 1)
                sp.dma_start(v_rows[:, v % NC, v // NC], stage[:, v % 4]).then_inc(st_v[v % 4], 16)
            for i in range(4):
                sp.wait_ge(st_v[i], 16 * (2 * NC // 4))
            load_v(0, 0, 0)

            def body(g, r, t):
                if is_last(g):
                    return
                if is_first(g):
                    sp.wait_ge(v_ready, 2 * NC)
                else:
                    sp.wait_ge(s_ready, KT * g)
                stacks(g - 1, 1 - r)
                if not is_first(g):
                    sp.wait_ge(pv_done, KT * g)
                load_v(g + 1, 1 - r, t + r)
                if r == 0 and more_weights(t):
                    sp.wait_ge(w_lo, t + 2)
                    load_w(t + 2)

            iterations(sp, body)
            o_rows = out.rearrange("b (n p) d -> p (b n) d", p=P)
            for n in range(NX):
                sp.wait_ge(o_res, n + 1)
                sp.dma_start(o_rows[:, n], osb[:, n % 4]).then_inc(st_o[n % 4], 16)
            for i in range(4):
                sp.wait_ge(st_o[i], 16 * (NX // 4))

        @block.gpsimd
        def _(pool):
            nc.gpsimd.memset(ident[:], 0.0).then_inc(zeroed, 1)
            nc.gpsimd.memset(mask[:], 0.0).then_inc(zeroed, 1)
            pool.wait_ge(zeroed, 2)
            nc.gpsimd.affine_select(out=ident[:], in_=ident[:], compare_op=ALU.not_equal, fill=1.0, base=0,
                                    pattern=[[-1, P]], channel_multiplier=1).then_inc(const, 1)
            nc.gpsimd.affine_select(out=mask[:], in_=mask[:], compare_op=ALU.not_equal, fill=1.0, base=0,
                                    pattern=[[-1, ROWS], [0, P]], channel_multiplier=1).then_inc(const, 1)
            nc.gpsimd.memset(ones[:], 1.0).then_inc(const, 1)
            nc.gpsimd.memset(half[:], -0.5).then_inc(const, 1)
            pool.wait_ge(sq_done, NX)
            nc.gpsimd.tensor_scalar(rstd[:], ssq[:], 1.0 / D, EPS, ALU.mult, ALU.add).then_inc(ms_done, 1)
            pool.wait_ge(ms_done, 1)
            pool.wait_ge(const, 4)
            nc.gpsimd.tensor_tensor(rstd[:], rstd[:], half[:], ALU.pow).then_inc(rstd_done, 1)

            def body(g, r, t):
                pool.wait_ge(p_ready, KT * g + 2)
                if not is_first(g):
                    pool.wait_ge(add_dve, DVE_ADDS * g)
                nc.gpsimd.tensor_tensor(accp[:], probs[:, 0], probs[:, 1], ALU.add).then_inc(add_pool, 1)
                for s in range(2, POOLED):
                    pool.wait_ge(p_ready, KT * g + s + 1)
                    pool.wait_ge(add_pool, POOL_ADDS * g + s - 1)
                    nc.gpsimd.tensor_tensor(accp[:], accp[:], probs[:, s % NP], ALU.add).then_inc(add_pool, 1)

            iterations(pool, body)

        @block.scalar
        def _(act):
            act.wait_ge(ld_x, 16)
            for n in range(NX):
                nc.scalar.activation(xn[:, n], xres[:, n], ACT.Square,
                                     accum_out=ssq[:, n:n + 1]).then_inc(sq_done, 1)
            act.wait_ge(ld_wv, 16)
            nc.scalar.copy(wv_hl[0], wv_raw).then_inc(wv_hi, 1)

            def split_w_hi(t):
                act.wait_ge(ld_w, 32 * (t + 1))
                nc.scalar.copy(wT[:, 0], wraw[:]).then_inc(w_hi, 1)

            split_w_hi(0)
            for u in range(2 * NC // 4):
                grp, c = u // DC, u % DC
                act.wait_ge(tr_ready, u + 1)
                nc.scalar.copy(cT[:, 0, c, BANK * grp:BANK * grp + BANK], ps[:, u % 4, :]).then_inc(tr_hi, 1)
            act.wait_ge(ld_nw, 16)
            for u in range(2 * NX // 4):
                grp, c = u // DC, u % DC
                n = u + 2 * NC // 4
                act.wait_ge(tr_ready, n + 1)
                nc.scalar.activation(xT[:, 0, c, BANK * grp:BANK * grp + BANK], ps[:, n % 4, :], ACT.Copy,
                                     scale=nw[:, c:c + 1]).then_inc(tr_hi, 1)

            def hi(g, what, i=0):
                bank, u = aux(g, what, i)
                act.wait_ge(aux_ready, u + 1)
                if not (isinstance(g, int) and g == -2):
                    for j in range(2):
                        act.wait_ge(st_j[j], STACKED * (g + 2))
                    if what == "k":
                        act.wait_ge(st_2, STACKED2 * (g + 2))
                dst = khl[:, 0, BANK * i:BANK * i + BANK] if what == "k" else qhl[:, 0, :]
                nc.scalar.copy(dst, bank).then_inc(hi_done, 1)

            for what, i in PROJECTIONS:
                hi(-2, what, i)
            for v in range(0, 2 * NC, 2):
                act.wait_ge(v_ready, v + 1)
                if v >= 4:
                    act.wait_ge(st_v[v % 4], 16 * (v // 4))
                nc.scalar.copy(stage[:, v % 4], ps[:, v % 4, :]).then_inc(v_act, 1)

            for what, i in PROJECTIONS:
                hi(-1, what, i)
            split_w_hi(1)
            for i in range(4):
                act.wait_ge(st_v[i], 16 * (2 * NC // 4))

            def exp(g, s):
                act.wait_ge(s_ready, KT * g + s + 1)
                first = is_first(g)
                if s >= 4 or not first:
                    act.wait_ge(pv_done, KT * g + s - 3)
                prev = s - NP if s >= NP else s - NP + KT
                if s >= NP or not first:
                    h = g if s >= NP else g - 1
                    if prev < POOLED:
                        act.wait_ge(add_pool, POOL_ADDS * h + max(1, prev))
                    else:
                        act.wait_ge(add_dve, DVE_ADDS * h + max(1, prev - POOLED))
                nc.scalar.activation(probs[:, s % NP], S[s % 2], ACT.Exp).then_inc(p_ready, 1)

            def evacuate(g, r, t):
                act.wait_ge(pv_done, KT * g)
                nc.scalar.copy(ctxT[:, 1 - r, t + r - 1, :], PV).then_inc(ctx_evac, 1)

            def body(g, r, t):
                last = is_last(g)
                for s in range(KT):
                    exp(g, s)
                    if s == 0:
                        if not is_first(g):
                            evacuate(g, r, t)
                        if last:
                            act.wait_ge(ld_wo, 16)
                            nc.scalar.copy(wo_hl[:, 0], wo_raw[:]).then_inc(wo_hi, 1)
                    for what, i in PLAN[s]:
                        if what in ("k", "q") and has(g, what):
                            hi(g, what, i)
                    if s == 7 and r == 1 and more_weights(t):
                        split_w_hi(t + 2)
                    if s >= 3 and last:
                        for n in range((s - 3) * NT // 5, (s - 2) * NT // 5):
                            o_hi_split(0, n)

            def o_hi_split(b, n):
                act.wait_ge(norm_done, 2 * n + b + 1)
                nc.scalar.copy(o_split(b, n)[0], ctxT[:, b, n, :]).then_inc(o_hi, 1)

            iterations(act, body)
            for n in range(NT - 1):
                o_hi_split(1, n)
            evacuate(NG, 0, NT)
            o_hi_split(1, NT - 1)

        @block.vector
        def _(dve):
            def const_rows(r):
                nc.vector.memset(kst[DK:P, r, 1].bitcast(fp32), 0.0).then_inc(rows_k, 1)
                dve.wait_ge(rows_k, 1 + 2 * r)
                nc.vector.memset(kst[DK:DK + ROWS, r, 1].bitcast(fp32), -1.0).then_inc(rows_k, 1)

            const_rows(0)
            nc.vector.memset(qst[DK:P, :, 1].bitcast(fp32), 0.0).then_inc(rows_q, 1)
            dve.wait_ge(rstd_done, 1)
            for n in range(NX):
                nc.vector.tensor_scalar(xn[:, n], xres[:, n], rstd[:, n:n + 1], None, ALU.mult).then_inc(xn_done, 1)
            dve.wait_ge(wv_hi, 1)
            nc.vector.tensor_tensor(wv_hl[1], wv_raw, wv_hl[0].bitcast(fp32), ALU.subtract).then_inc(wv_lo, 1)

            def split_w_lo(t):
                dve.wait_ge(w_hi, t + 1)
                nc.vector.tensor_tensor(wT[:, 1], wraw[:], wT[:, 0].bitcast(fp32), ALU.subtract).then_inc(w_lo, 1)

            split_w_lo(0)
            for u in range(2 * NC // 4):
                grp, c = u // DC, u % DC
                cols = slice(BANK * grp, BANK * grp + BANK)
                dve.wait_ge(tr_hi, u + 1)
                nc.vector.tensor_tensor(cT[:, 1, c, cols], ps[:, u % 4, :], cT[:, 0, c, cols].bitcast(fp32),
                                        ALU.subtract).then_inc(tr_lo, 1)
            for u in range(2 * NX // 4):
                grp, c = u // DC, u % DC
                n = u + 2 * NC // 4
                cols = slice(BANK * grp, BANK * grp + BANK)
                dve.wait_ge(tr_hi, n + 1)
                nc.vector.scalar_tensor_tensor(out=xT[:, 1, c, cols], in0=ps[:, n % 4, :], scalar=nw[:, c:c + 1],
                                               in1=xT[:, 0, c, cols].bitcast(fp32), op0=ALU.mult,
                                               op1=ALU.subtract).then_inc(tr_lo, 1)

            def lo(g, what, i=0):
                bank, _ = aux(g, what, i)
                t = khl if what == "k" else qhl
                cols = slice(BANK * i, BANK * i + BANK)
                dve.wait_ge(hi_done, 3 * (g + 2) + PROJECTIONS.index((what, i)) + 1)
                nc.vector.tensor_tensor(t[:, 1, cols], bank, t[:, 0, cols].bitcast(fp32),
                                        ALU.subtract).then_inc(aux_free, 1)

            def reduce(g, i):
                bank, u = aux(g, "max", i)
                dve.wait_ge(aux_ready, u + 1)
                nc.vector.reduce_max(mpart[:, i // KH_, i % KH_:i % KH_ + 1], bank, AX.X).then_inc(aux_free, 1)

            def combine(g):
                dve.wait_ge(aux_free, aux(g, "max", NMAX - 1)[1] + 1)
                nc.vector.reduce_max(mcol[:], mpart[:], AX.X).then_inc(mcol_ready, 1)

            def spread(g, r):
                bank, u = aux(g, "maxT")
                dve.wait_ge(aux_ready, u + 1)
                dst = qst[DK:DK + ROWS, r, 1].rearrange("p j (n q) -> p (j n) q", q=P)
                src = bank[0:ROWS, 0:P].unsqueeze(1).to_broadcast([ROWS, ROWS, P])
                nc.vector.tensor_tensor(dst, src, mask[:], ALU.mult).then_inc(aux_free, 1)

            for what, i in PROJECTIONS:
                lo(-2, what, i)
            i = 0
            for v in range(2 * NC):
                if v >= NC and i < NMAX:
                    reduce(-1, i)
                    i += 1
                if v % 2 == 1:
                    dve.wait_ge(v_ready, v + 1)
                    if v >= 4:
                        dve.wait_ge(st_v[v % 4], 16 * (v // 4))
                    nc.vector.tensor_copy(stage[:, v % 4], ps[:, v % 4, :]).then_inc(v_dve, 1)
            combine(-1)
            dve.wait_ge(const, 4)
            dve.wait_ge(rows_q, 1)
            spread(-1, 0)
            for what, i in PROJECTIONS:
                lo(-1, what, i)
            split_w_lo(1)
            const_rows(1)

            def add(g, k):
                if k > 0:
                    dve.wait_ge(add_dve, DVE_ADDS * g + k)
                if k < DVE_ADDS - 1:
                    s = POOLED + 1 + k
                    dve.wait_ge(p_ready, KT * g + s + 1)
                    ins = acc[:] if k > 0 else probs[:, POOLED % NP], probs[:, s % NP]
                else:
                    dve.wait_ge(add_pool, POOL_ADDS * (g + 1))
                    ins = acc[:], accp[:]
                nc.vector.tensor_tensor(acc[:], ins[0], ins[1], ALU.add).then_inc(add_dve, 1)

            def normalise(g, unit, b, n):
                bank, u = unit
                dve.wait_ge(aux_ready, u + 1)
                nc.vector.reciprocal(rec[:], bank).then_inc(aux_free, 1)
                dve.wait_ge(ctx_evac, g)
                dve.wait_ge(aux_free, DENS_FREE if isinstance(g, int) and g == NG else u + 1)
                nc.vector.tensor_tensor(ctxT[:, b, n, :], ctxT[:, b, n, :], rec[:], ALU.mult).then_inc(norm_done, 1)

            def o_lo_split(b, n):
                dve.wait_ge(o_hi, b * NT + n + 1)
                h, l = o_split(b, n)
                nc.vector.tensor_tensor(l, ctxT[:, b, n, :], h.bitcast(fp32), ALU.subtract).then_inc(o_lo, 1)

            def residual(n, unit):
                bank, u = unit
                dve.wait_ge(aux_ready, u + 1)
                if n >= 4:
                    dve.wait_ge(st_o[n % 4], 16 * (n // 4))
                nc.vector.tensor_tensor(osb[:, n % 4], bank[:, 0:D], xres[:, n], ALU.add).then_inc(o_res, 1)

            def body(g, r, t):
                last = is_last(g)
                if not is_first(g):
                    add(g - 1, 1)
                    add(g - 1, 2)
                for s in range(KT):
                    for what, i in PLAN[s]:
                        if not has(g, what):
                            continue
                        if what == "max":
                            reduce(g, i)
                        elif what == "den":
                            normalise(g, tail(DEN_PREV) if last else aux(g, "den"), 1 - r, t + r - 1)
                        elif what == "maxT":
                            spread(g, 1 - r)
                        else:
                            lo(g, what, i)
                    if s == 3 and last:
                        dve.wait_ge(wo_hi, 1)
                        nc.vector.tensor_tensor(wo_hl[:, 1], wo_raw[:], wo_hl[:, 0].bitcast(fp32),
                                                ALU.subtract).then_inc(wo_lo, 1)
                    if s == 5:
                        if last:
                            for n in range(NT // 2):
                                o_lo_split(0, n)
                        else:
                            combine(g)
                if last:
                    for n in range(NT // 2, NT):
                        o_lo_split(0, n)
                add(g, 0)
                if r == 1 and more_weights(t):
                    split_w_lo(t + 2)

            iterations(dve, body)
            add(NG - 1, 1)
            add(NG - 1, 2)
            for n in range(QT):
                residual(n, tail(WO0 + n))
            for n in range(NT - 1):
                o_lo_split(1, n)
            normalise(NG, tail(DEN_LAST), 1, NT - 1)
            o_lo_split(1, NT - 1)
            for n in range(QT):
                residual(QT + n, tail(WO1 + n))

        @block.tensor
        def _(pe):
            mm = nc.tensor.matmul

            pe.wait_ge(const, 1)
            for u in range(2 * (NC + NX) // 4):
                if u < 2 * NC // 4:
                    src, grp, c = craw, u // DC, u % DC
                    pe.wait_ge(ld_c[grp], 16)
                else:
                    src, grp, c = xn, (u - 2 * NC // 4) // DC, u % DC
                    pe.wait_ge(xn_done, NX)
                if u >= 4:
                    pe.wait_ge(tr_lo, u - 3)
                for i in range(4):
                    last = nc.tensor.transpose(ps[:, u % 4, P * i:P * i + P],
                                               src[:, 4 * grp + i, P * c:P * c + P], ident[:])
                last.then_inc(tr_ready, 1)
            pe.wait_ge(tr_lo, 2 * (NC + NX) // 4)

            def aux_wait(u):
                if not (isinstance(u, int) and u < 3):
                    pe.wait_ge(aux_free, u - 2)

            def split_product(bank, lhs, rhs, chunks):
                terms = [(h, l, c) for c in range(chunks) for h, l in ((0, 0), (0, 1), (1, 0))]
                for i, (h, l, c) in enumerate(terms):
                    last = mm(bank, lhs(h, c), rhs(l, c), start=(i == 0), stop=(i == len(terms) - 1))
                return last

            def project(g, what, i, b):
                bank, u = aux(g, what, i)
                aux_wait(u)
                m = 1 if what == "k" else 0
                src, col = (cT, KV * b + BANK * i) if what == "k" else (xT, Q * b)
                split_product(bank, lambda h, c: wT[:, h, m, c], lambda h, c: src[:, h, c, col:col + BANK],
                              DC).then_inc(aux_ready, 1)

            def approx_scores(g, r, i):
                bank, u = aux(g, "max", i)
                j, q, k = i // (QT * KH_), i // KH_ % QT, i % KH_
                aux_wait(u)
                mm(bank, qst[:, r, 0, j, P * q:P * q + P], kst[:, r, 0, j, BANK * k:BANK * k + BANK],
                   start=True, stop=True).then_inc(aux_ready, 1)

            def max_rows(g):
                bank, u = aux(g, "maxT")
                pe.wait_ge(mcol_ready, g + 2)
                aux_wait(u)
                nc.tensor.transpose(bank[0:ROWS, 0:P], mcol[:], ident[:]).then_inc(aux_ready, 1)

            def scores(g, r, s):
                buf = S[s % 2]
                if not (is_first(g) and s < 2):
                    pe.wait_ge(p_ready, KT * g + s - 1)
                keys = slice(P * s, P * s + P)
                for j in range(2):
                    mm(buf[:, j], kst[:, r, 0, j, keys], qst[:, r, 0, j], start=True, stop=False)
                if s == 0:
                    pe.wait_ge(aux_free, aux(g - 1, "maxT")[1] + 1)
                    pe.wait_ge(st_2, STACKED2 * (g + 1))
                    if is_first(g):
                        pe.wait_ge(rows_k, 2)
                    if isinstance(g, int) and g == 1:
                        pe.wait_ge(rows_k, 4)
                for j in range(2):
                    last = mm(buf[:, j], kst[:, r, 1, j, keys], qst[:, r, 1, j], start=False, stop=True)
                last.then_inc(s_ready, 1)

            def values(g, r, s, t):
                pe.wait_ge(p_ready, KT * g + s + 1)
                if s == 0:
                    pe.wait_ge(ld_v[r], 16 * (t + 1))
                    if not is_first(g):
                        pe.wait_ge(ctx_evac, g)
                for j in range(2):
                    rows = slice(DK * j, DK * j + DK)
                    last = mm(PV[rows, :], vals[:, r, s, rows], probs[:, s % NP, j],
                              start=(s == 0), stop=(s == KT - 1))
                last.then_inc(pv_done, 1)

            def denominators(g, unit):
                bank, u = unit
                pe.wait_ge(add_dve, DVE_ADDS * g)
                if isinstance(g, int) and g == NG:
                    tail_wait(DEN_LAST)
                else:
                    aux_wait(u)
                for j in range(2):
                    last = mm(bank[DK * j:DK * j + DK, :], ones[:], acc[:, j], start=True, stop=True)
                last.then_inc(aux_ready, 1)

            def tail_wait(i):
                if i - 3 <= DEN_PREV:
                    pe.wait_ge(aux_free, TAIL + i - 2)
                elif i - 3 == DEN_LAST:
                    pe.wait_ge(aux_free, DENS_FREE)
                else:
                    pe.wait_ge(o_res, i - 3 - WO0 + 1 - (i - 3 > DEN_LAST))

            def output(b, n, i):
                bank, _ = tail(i)
                tail_wait(i)
                rows = slice(P * n, P * n + P)
                split_product(bank[:, 0:D], lambda h, c: o_split(b, c)[h][:, rows], lambda l, c: wo_hl[:, l, c],
                              NT).then_inc(aux_ready, 1)

            pe.wait_ge(w_lo, 1)
            for what, i in PROJECTIONS:
                project(-2, what, i, 0)
            pe.wait_ge(wv_lo, 1)
            i = 0
            for v in range(2 * NC):
                if v >= 4:
                    pe.wait_ge(v_act if v % 2 == 0 else v_dve, (v - 4) // 2 + 1)
                rows = slice(P * (v % NC), P * (v % NC) + P)
                cols = slice(BANK * (v // NC), BANK * (v // NC) + BANK)
                split_product(ps[:, v % 4, :], lambda h, c: cT[:, h, c, rows], lambda l, c: wv_hl[l][:, c, cols],
                              DC).then_inc(v_ready, 1)
                if v >= NC and i < NMAX:
                    if i % (NMAX // 2) == 0:
                        pe.wait_ge(st_j[2 * i // NMAX], STACKED)
                    approx_scores(-1, 0, i)
                    i += 1
            max_rows(-1)
            for what, i in PROJECTIONS:
                project(-1, what, i, 1)
            pe.wait_ge(v_act, NC)
            pe.wait_ge(v_dve, NC)

            def body(g, r, t):
                last = is_last(g)
                for s in range(KT):
                    scores(g, r, s)
                    if s > 0:
                        values(g, r, s - 1, t)
                    elif not is_first(g):
                        values(g - 1, 1 - r, KT - 1, t + r - 1)
                    for what, i in PLAN[s]:
                        if not has(g, what):
                            continue
                        if what == "max":
                            if i % (NMAX // 2) == 0:
                                pe.wait_ge(st_j[2 * i // NMAX], STACKED * (g + 2))
                            approx_scores(g, 1 - r, i)
                        elif what == "maxT":
                            max_rows(g)
                        elif what == "den":
                            denominators(g, tail(DEN_PREV) if last else aux(g, "den"))
                        else:
                            pe.wait_ge(w_lo, t + 2)
                            project(g, what, i, r)

            iterations(pe, body)
            values(NG - 1, 1, KT - 1, NT - 1)
            pe.wait_ge(wo_lo, 1)
            pe.wait_ge(o_lo, NT)
            for n in range(QT):
                output(0, n, WO0 + n)
            denominators(NG, tail(DEN_LAST))
            pe.wait_ge(o_lo, 2 * NT)
            for n in range(QT):
                output(1, n, WO1 + n)


_INS = ['x', 'ctx_1024', 'L0_xattn_wq', 'L0_xattn_wk', 'L0_xattn_wv', 'L0_xattn_wo', 'L0_xattn_norm_w']


def kernel(**inputs):
    import numpy as _np
    import concourse.bacc as _bacc
    from concourse import mybir as _mybir
    from concourse.bass_utils import run_bass_kernel_spmd as _run

    nc = _bacc.Bacc("TRN2", target_bir_lowering=False, num_devices=1)
    arrays, args = {}, []
    for name in _INS:
        a = _np.ascontiguousarray(inputs[name])
        arrays[f"in_{name}"] = a
        args.append(nc.dram_tensor(f"in_{name}", a.shape, _mybir.dt.from_np(a.dtype), kind="ExternalInput").ap())
    args.append(nc.dram_tensor("out_0", tuple(inputs['x'].shape), _mybir.dt.float32, kind="ExternalOutput").ap())
    cross_attention_program(nc, *args)
    r = _run(nc, [arrays], core_ids=[0])
    return r.results[0]["out_0"]
```

```python
import concourse.bass as bass
from concourse import mybir
from contextlib import ExitStack


def cross_attention_program(nc, x, ctx_in, wq, wk, wv, wo, norm_w, out):
    fp32 = mybir.dt.float32
    f32r = mybir.dt.float32r
    ALU = mybir.AluOpType
    ACT = mybir.ActivationFunctionType
    AX = mybir.AxisListType

    P = 128
    B, Q, D = x.shape
    KV = ctx_in.shape[1]
    INNER = wq.shape[1]
    DK = 64
    EPS = 1e-6
    NT = INNER // P
    NG = B * NT
    DC = D // P
    KT = KV // P
    QT = Q // P
    BANK = 512
    KH = KV // BANK
    NX = B * Q // P
    NC = B * KV // P
    XU = NX * DC // 4
    CU = NC * DC // 4
    NP = 4
    ROWS = 2 * QT
    NMAX = 2 * QT * KH

    ctx = ExitStack()
    with ctx:
        def sb(name, shape, dt):
            return ctx.enter_context(nc.sbuf_tensor(name, shape, dt))

        def sem(name):
            return ctx.enter_context(nc.semaphore(name))

        cT = sb("cT", [P, 2, DC, B * KV], f32r)
        xT = sb("xT", [P, 2, DC, B * Q], f32r)
        wT = sb("w_split", [P, 2, 2, DC, P], f32r)
        kst = sb("k_stacks", [P, 2, 2, 2, KV], f32r)
        qst = sb("q_stacks", [P, 2, 2, 2, Q], f32r)
        khl = sb("k_split", [P, 2, KV], f32r)
        qhl = sb("q_split", [P, 2, Q], f32r)
        ctxT = sb("ctxT", [P, B, NT, Q], fp32)
        probs = sb("probs", [P, NP, 2, Q], fp32)
        vals = sb("vals", [P, 2, KT, P], fp32)
        wraw = sb("w_raw", [P, 2, DC, P], fp32)
        acc = sb("acc", [P, 2, Q], fp32)
        accp = sb("acc_pool", [P, 2, Q], fp32)
        rec = sb("rec", [P, Q], fp32)
        xres = sb("xres", [P, NX, D], fp32)
        wo_raw = sb("wo_raw", [P, NT, D], fp32)
        osb = sb("osb", [P, 4, D], fp32)
        mask = sb("mask", [ROWS, ROWS, P], fp32)
        ident = sb("ident", [P, P], fp32)
        ones = sb("ones", [P, DK], fp32)
        nw = sb("nw", [P, DC], fp32)
        ssq = sb("ssq", [P, NX], fp32)
        rstd = sb("rstd", [P, NX], fp32)
        half = sb("minus_half", [P, NX], fp32)
        mpart = sb("mpart", [P, 2 * QT, KH], fp32)
        mcol = sb("mcol", [P, 2 * QT], fp32)
        v_dram = nc.dram_tensor("v_scratch", [B * KV, INNER], fp32, kind="Internal").ap()

        craw = ctxT[:, 0, :, :].rearrange("p a (b d) -> p (a b) d", d=D)
        xn = ctxT[:, 1, 0:NX * D // Q, :].rearrange("p a (b d) -> p (a b) d", d=D)
        wv_raw = probs[:, 0:2].rearrange("p s j q -> p s (j q)")
        stage = probs[:, 2:4].rearrange("p s j q -> p (s j) q")
        wv_hl = [kst[:, 1, i].rearrange("p j k -> p (j k)").rearrange("p (c n) -> p c n", c=DC)
                 for i in range(2)]
        wo_hl = xT[:].rearrange("p h c t -> p h (c t)").rearrange("p h (n d) -> p h n d", d=D)
        o0 = cT[:].rearrange("p h c t -> p h (c t)").rearrange("p h (n q) -> p h n q", q=Q)
        o1_hi = kst[:, 0].rearrange("p s j k -> p (s j k)").rearrange("p (n q) -> p n q", q=Q)
        o1_lo = [qst[:, 0].rearrange("p s j q -> p (s j) q"),
                 khl[:].rearrange("p h k -> p (h k)").rearrange("p (n q) -> p n q", q=Q)]

        def o_split(b, n):
            if b == 0:
                return o0[:, 0, n, :], o0[:, 1, n, :]
            return o1_hi[:, n, :], o1_lo[n // 4][:, n % 4, :]

        ps = ctx.enter_context(nc.psum_tensor("ps", [P, 8, BANK], fp32))
        S = [ps[:, 0:2, :], ps[:, 2:4, :]]
        PV = ps[:, 4, :]
        AUX = [ps[:, 5, :], ps[:, 6, :], ps[:, 7, :]]

        def transposed(u):
            return ps[:, u, :] if u < 4 else [PV, AUX[2]][u % 2]

        ld_x = sem("ld_x")
        ld_c = [sem(f"ld_c{i}") for i in range(4)]
        ld_nw = sem("ld_nw")
        ld_wv = sem("ld_wv")
        ld_wo = sem("ld_wo")
        ld_w = sem("ld_w")
        ld_v = [sem(f"ld_v{i}") for i in range(2)]
        st_v = [sem(f"st_v{i}") for i in range(4)]
        st_o = [sem(f"st_o{i}") for i in range(4)]
        const = sem("const")
        sq_done = sem("sq_done")
        ms_done = sem("ms_done")
        rstd_done = sem("rstd_done")
        xn_done = sem("xn_done")
        tr_ready = sem("tr_ready")
        tr_hi = sem("tr_hi")
        tr_lo = sem("tr_lo")
        wv_hi = sem("wv_hi")
        wv_lo = sem("wv_lo")
        w_hi = sem("w_hi")
        w_lo = sem("w_lo")
        v_ready = sem("v_ready")
        v_act = sem("v_act")
        v_dve = sem("v_dve")
        aux_ready = sem("aux_ready")
        aux_free = sem("aux_free")
        hi_done = sem("hi_done")
        st_k0 = sem("st_k0")
        st_k1 = [sem(f"st_k1_{j}") for j in range(2)]
        st_q = [sem(f"st_q{j}") for j in range(2)]
        mcol_ready = sem("mcol_ready")
        s_ready = sem("s_ready")
        p_ready = sem("p_ready")
        pv_done = sem("pv_done")
        ctx_evac = sem("ctx_evac")
        norm_done = sem("norm_done")
        sum_done = sem("sum_done")
        add_pool = sem("add_pool")
        wo_hi = sem("wo_hi")
        wo_lo = sem("wo_lo")
        o_hi = sem("o_hi")
        o_lo = sem("o_lo")
        o_res = sem("o_res")
        zeroed = sem("zeroed")
        rows_k0 = sem("rows_k0")
        rows_k1 = sem("rows_k1")
        rows_q = sem("rows_q")

        PLAN = [
            [], [],
            [("den", 0)], [("k", 0)],
            [("max", 0)], [("max", 1), ("max", 2)],
            [("max", 3), ("max", 4)], [("max", 5), ("max", 6)],
            [("k", 1)], [("max", 7), ("max", 8)],
            [("max", 9), ("max", 10)], [("max", 11), ("max", 12)],
            [("max", 13), ("max", 14)], [("max", 15)],
            [], [("maxT", 0), ("q", 0)],
        ]

        def max_unit(i):
            return i // (QT * KH), i // QT % KH, i % QT

        PROJECTIONS = [("k", 0), ("k", 1), ("q", 0)]
        UNITS = [u for units in PLAN for u in units]
        PER = len(UNITS)

        def has(g, what):
            if not isinstance(g, int):
                return True
            return {"den": g >= 1, "k": g < NG - 2, "q": g < NG - 2, "max": g < NG - 1, "maxT": g < NG - 1}[what]

        def order(g):
            if g == -2:
                return PROJECTIONS
            if g == -1:
                return [("max", i) for i in range(NMAX)] + [("k", 0), ("k", 1), ("maxT", 0), ("q", 0)]
            return [u for u in UNITS if has(g, u[0])]

        def before(g):
            return sum(len(order(h)) for h in range(-2, g))

        def aux(g, what, i=0):
            if isinstance(g, int):
                n = before(g) + order(g).index((what, i))
                return AUX[n % 3], n
            n = before(2) - 2 * PER + UNITS.index((what, i))
            return AUX[n % 3], PER * g + n

        TAIL = before(NG - 1)

        def tail(i):
            return AUX[(TAIL + i) % 3], TAIL + i

        DEN_PREV, WO0, DEN_LAST = 0, 1, 3
        TAIL_UNITS = 1 + NX + 1
        DENS_FREE = TAIL + 2

        AFTER_V = [[] for _ in range(2 * NC)]
        AFTER_V[0] = [("T", 6), ("square", 0)]
        AFTER_V[1] = [("T", 7)]
        AFTER_V[5] = [("norm", 0)]
        for i in range(XU):
            AFTER_V[8 + i] = [("T", CU + i)]
        AFTER_V[13] = [("q", -2)]
        for i in range(NMAX):
            AFTER_V[18 + i * 11 // NMAX] += [("max", i)]
        AFTER_V[29] = [("k", -1)]

        def iterations(eng, body):
            body(0, 0, 0)
            body(1, 1, 0)
            with eng.Fori(1, NT - 2) as t:
                body(2 * t, 0, t)
                body(2 * t + 1, 1, t)
            body(NG - 4, 0, NT - 2)
            body(NG - 3, 1, NT - 2)
            body(NG - 2, 0, NT - 1)
            body(NG - 1, 1, NT - 1)

        def more_weights(t):
            return not isinstance(t, int) or t + 2 < NT

        def is_int(g, n):
            return isinstance(g, int) and g == n

        def is_last(g):
            return isinstance(g, int) and g == NG - 1

        def is_first(g):
            return isinstance(g, int) and g == 0

        POOL_ADDS = KT - 2
        STACKED = 2 * 16
        STACKED_K0 = 2 * STACKED
        SPLITS = {
            (NG - 1, 0): [(0, 0), (0, 1), (0, 2)], (NG - 1, 1): [(0, 3), (0, 4)], (NG - 1, 2): [(0, 5), (0, 6)],
            (NG - 1, 4): [(0, 7), (1, 0)], (NG - 1, 5): [(1, 1), (1, 2)], (NG - 1, 6): [(1, 3), (1, 4)],
            (NG - 1, 7): [(1, 5), (1, 6)],
        }
        WO_PARTS = [0, 3]

        def splits(g, s):
            return SPLITS.get((g, s), []) if isinstance(g, int) else []

        def wo_part(g, s):
            if not (is_int(g, NG - 2) and s in WO_PARTS):
                return None
            n = NT // len(WO_PARTS)
            return slice(n * WO_PARTS.index(s), n * WO_PARTS.index(s) + n)

        block = ctx.enter_context(nc.Block())

        def w_columns(w, t):
            return w.rearrange("(c p) (n m) -> p c n m", p=P, m=P)[:, :, t, :]

        @block.sync
        def _(sp):
            def load_w(t):
                sp.dma_start(wraw[:, 0], w_columns(wq, t)).then_inc(ld_w, 16)
                sp.dma_start(wraw[:, 1], w_columns(wk, t)).then_inc(ld_w, 16)

            x_rows = x.rearrange("b (n p) d -> p (b n) d", p=P)
            c_rows = ctx_in.rearrange("b (n p) d -> p (b n) d", p=P)
            for i in range(4):
                sp.dma_start(craw[:, 4 * i:4 * i + 4], c_rows[:, 4 * i:4 * i + 4]).then_inc(ld_c[i], 16)
                if i == 0:
                    load_w(0)
                if i == 1:
                    sp.dma_start(wv_raw, wv.rearrange("(c p) n -> p c n", p=P)).then_inc(ld_wv, 16)
            sp.dma_start(xres[:], x_rows).then_inc(ld_x, 16)
            with nc.allow_non_contiguous_dma(reason="256 scales, one per partition and chunk"):
                sp.dma_start(nw[:], norm_w.rearrange("(c p) -> p c", p=P)).then_inc(ld_nw, 16)
            sp.dma_start(wo_raw[:], wo.rearrange("(n p) d -> p n d", p=P)).then_inc(ld_wo, 16)

            def copy(dst, src, done):
                sp.dma_start(dst.bitcast(fp32), src.bitcast(fp32)).then_inc(done, 16)

            def stack_keys(r, j, k, done):
                rows, cols = slice(DK * j, DK * j + DK), slice(BANK * k, BANK * k + BANK)
                hi_twice = khl[rows, 0, cols].unsqueeze(1).to_broadcast([DK, 2, BANK])
                copy(kst[0:DK, r, :, j, cols], hi_twice, done)
                copy(kst[DK:P, r, 0, j, cols], khl[rows, 1, cols], done)

            def stack_first_keys(r):
                for j in range(2):
                    stack_keys(r, j, 0, st_k0)

            def stack_queries(r, j):
                rows = slice(DK * j, DK * j + DK)
                copy(qst[DK:P, r, 0, j], qhl[rows, 0], st_q[j])
                copy(qst[0:DK, r, :, j], qhl[rows], st_q[j])

            def stack_rest(r):
                for j in range(2):
                    stack_queries(r, j)
                    stack_keys(r, j, 1, st_k1[j])

            def load_v(g, r, t):
                src = v_dram.rearrange("(b k p) (n m) -> p b k n m", p=P, k=KT, m=P)[:, r, :, t, :]
                sp.dma_start(vals[:, r], src).then_inc(ld_v[r], 16)

            v_rows = v_dram.rearrange("(n p) (h c) -> p n h c", p=P, c=BANK)
            for v in range(2 * NC):
                sp.wait_ge(v_act if v % 2 == 0 else v_dve, v // 2 + 1)
                sp.dma_start(v_rows[:, v % NC, v // NC], stage[:, v % 4]).then_inc(st_v[v % 4], 16)
                if v == 3:
                    sp.wait_ge(aux_free, aux(-2, "k", 1)[1] + 1)
                    stack_first_keys(0)
                if v == 5:
                    for j in range(2):
                        stack_keys(0, j, 1, st_k1[j])
                if v == 7:
                    sp.wait_ge(w_lo, 1)
                    load_w(1)
                if v == 14:
                    sp.wait_ge(aux_free, aux(-2, "q")[1] + 1)
                    stack_queries(0, 0)
                if v == 16:
                    stack_queries(0, 1)
                if v == NC + 4:
                    for i in range(4):
                        sp.wait_ge(st_v[i], 16 * (NC // 4))
                    load_v(0, 0, 0)

            def body(g, r, t):
                if is_last(g):
                    return
                if is_first(g):
                    sp.wait_ge(v_ready, 2 * NC)
                    sp.wait_ge(aux_free, aux(-1, "k", 1)[1] + 1)
                    stack_first_keys(1)
                sp.wait_ge(aux_free, aux(g - 1, "q")[1] + 1)
                if not is_first(g):
                    sp.wait_ge(s_ready, KT * (g - 1) + KT if r == 0 else KT * g)
                stack_rest(1 - r)
                if is_first(g):
                    for i in range(4):
                        sp.wait_ge(st_v[i], 16 * (2 * NC // 4))
                else:
                    sp.wait_ge(pv_done, KT * g)
                load_v(g + 1, 1 - r, t + r)
                if r == 0 and more_weights(t):
                    sp.wait_ge(w_lo, t + 2)
                    load_w(t + 2)
                if has(g, "k"):
                    sp.wait_ge(s_ready, KT * g + KT // KH)
                    stack_first_keys(r)

            iterations(sp, body)
            o_rows = out.rearrange("b (n p) d -> p (b n) d", p=P)
            for n in range(NX):
                sp.wait_ge(o_res, n + 1)
                sp.dma_start(o_rows[:, n], osb[:, n % 4]).then_inc(st_o[n % 4], 16)
            for i in range(4):
                sp.wait_ge(st_o[i], 16 * (NX // 4))

        @block.gpsimd
        def _(pool):
            nc.gpsimd.memset(ident[:], 0.0).then_inc(zeroed, 1)
            nc.gpsimd.memset(mask[:], 0.0).then_inc(zeroed, 1)
            pool.wait_ge(zeroed, 2)
            nc.gpsimd.affine_select(out=ident[:], in_=ident[:], compare_op=ALU.not_equal, fill=1.0, base=0,
                                    pattern=[[-1, P]], channel_multiplier=1).then_inc(const, 1)
            nc.gpsimd.affine_select(out=mask[:], in_=mask[:], compare_op=ALU.not_equal, fill=1.0, base=0,
                                    pattern=[[-1, ROWS], [0, P]], channel_multiplier=1).then_inc(const, 1)
            nc.gpsimd.memset(ones[:], 1.0).then_inc(const, 1)
            nc.gpsimd.memset(half[:], -0.5).then_inc(const, 1)
            pool.wait_ge(const, 4)
            nc.gpsimd.memset(kst[DK:P, 0, 1].bitcast(fp32), 0.0).then_inc(rows_k0, 1)
            pool.wait_ge(rows_k0, 1)
            nc.gpsimd.memset(kst[DK:DK + ROWS, 0, 1].bitcast(fp32), -1.0).then_inc(rows_k0, 1)
            pool.wait_ge(rows_k0, 2)
            nc.gpsimd.memset(qst[DK:P, :, 1].bitcast(fp32), 0.0).then_inc(rows_q, 1)
            pool.wait_ge(rows_q, 1)
            pool.wait_ge(sq_done, NX)
            nc.gpsimd.tensor_scalar(rstd[:], ssq[:], 1.0 / D, EPS, ALU.mult, ALU.add).then_inc(ms_done, 1)
            pool.wait_ge(ms_done, 1)
            pool.wait_ge(const, 4)
            nc.gpsimd.tensor_tensor(rstd[:], rstd[:], half[:], ALU.pow).then_inc(rstd_done, 1)

            pool.wait_ge(v_ready, 2 * NC)
            nc.gpsimd.memset(kst[DK:P, 1, 1].bitcast(fp32), 0.0).then_inc(rows_k1, 1)
            pool.wait_ge(rows_k1, 1)
            nc.gpsimd.memset(kst[DK:DK + ROWS, 1, 1].bitcast(fp32), -1.0).then_inc(rows_k1, 1)
            pool.wait_ge(rows_k1, 2)

            def body(g, r, t):
                pool.wait_ge(p_ready, KT * g + 2)
                if not is_first(g):
                    pool.wait_ge(sum_done, g)
                nc.gpsimd.tensor_tensor(accp[:], probs[:, 0], probs[:, 1], ALU.add).then_inc(add_pool, 1)
                for s in range(2, KT - 1):
                    pool.wait_ge(p_ready, KT * g + s + 1)
                    pool.wait_ge(add_pool, POOL_ADDS * g + s - 1)
                    nc.gpsimd.tensor_tensor(accp[:], accp[:], probs[:, s % NP], ALU.add).then_inc(add_pool, 1)

                if is_int(g, NG - 2):
                    pool.wait_ge(wo_hi, len(WO_PARTS))
                    pool.wait_ge(add_pool, POOL_ADDS * (g + 1))
                    nc.gpsimd.tensor_tensor(wo_hl[:, 1], wo_raw[:], wo_hl[:, 0].bitcast(fp32),
                                            ALU.subtract).then_inc(wo_lo, 1)

            iterations(pool, body)

        @block.scalar
        def _(act):
            def split_w_hi(t):
                act.wait_ge(ld_w, 32 * (t + 1))
                nc.scalar.copy(wT[:, 0], wraw[:]).then_inc(w_hi, 1)

            def transposed_hi(u):
                act.wait_ge(tr_ready, u + 1)
                dst, c, cols = (cT, u % DC, u // DC) if u < CU else (xT, u % DC, (u - CU) // DC)
                dst = dst[:, 0, c, BANK * cols:BANK * cols + BANK]
                if u < CU:
                    nc.scalar.copy(dst, transposed(u)).then_inc(tr_hi, 1)
                else:
                    act.wait_ge(ld_nw, 16)
                    nc.scalar.activation(dst, transposed(u), ACT.Copy, scale=nw[:, c:c + 1]).then_inc(tr_hi, 1)

            for u in range(4):
                if u == 2:
                    split_w_hi(0)
                transposed_hi(u)
            act.wait_ge(ld_wv, 16)
            for c in range(DC):
                nc.scalar.copy(wv_hl[0][:, c], wv_raw[:, c]).then_inc(wv_hi, 1)
            for u in (4, 5):
                transposed_hi(u)

            def hi(g, what, i=0):
                bank, u = aux(g, what, i)
                act.wait_ge(aux_ready, u + 1)
                if not (isinstance(g, int) and g == -2):
                    if (what, i) == ("k", 0):
                        act.wait_ge(st_k0, STACKED_K0 * (g + 2))
                    else:
                        for j in range(2):
                            act.wait_ge((st_k1 if what == "k" else st_q)[j], STACKED * (g + 2))
                dst = khl[:, 0, BANK * i:BANK * i + BANK] if what == "k" else qhl[:, 0, :]
                nc.scalar.copy(dst, bank).then_inc(hi_done, 1)

            for i in range(KH):
                hi(-2, "k", i)
            for v in range(2 * NC):
                if v % 2 == 0:
                    act.wait_ge(v_ready, v + 1)
                    if v >= 4:
                        act.wait_ge(st_v[v % 4], 16 * (v // 4))
                    nc.scalar.copy(stage[:, v % 4], ps[:, v % 4, :]).then_inc(v_act, 1)
                for what, i in AFTER_V[v]:
                    if what == "T":
                        transposed_hi(i)
                    elif what == "square":
                        act.wait_ge(ld_x, 16)
                        for n in range(NX):
                            nc.scalar.activation(xn[:, n], xres[:, n], ACT.Square,
                                                 accum_out=ssq[:, n:n + 1]).then_inc(sq_done, 1)
                    elif what == "q":
                        hi(i, "q")
                    elif what == "k":
                        for h in range(KH):
                            hi(i, "k", h)

            hi(-1, "q")
            split_w_hi(1)

            def exp(g, s):
                act.wait_ge(s_ready, KT * g + s + 1)
                first = is_first(g)
                if first and s == 2:
                    for i in range(4):
                        act.wait_ge(st_v[i], 16 * (2 * NC // 4))
                if s >= 4 or not first:
                    act.wait_ge(pv_done, KT * g + s - 3)
                prev = s - NP if s >= NP else s - NP + KT
                if s >= NP or not first:
                    h = g if s >= NP else g - 1
                    if prev < KT - 1:
                        act.wait_ge(add_pool, POOL_ADDS * h + max(1, prev))
                    else:
                        act.wait_ge(sum_done, h + 1)
                nc.scalar.activation(probs[:, s % NP], S[s % 2], ACT.Exp).then_inc(p_ready, 1)

            def evacuate(g, r, t):
                act.wait_ge(pv_done, KT * g)
                nc.scalar.copy(ctxT[:, 1 - r, t + r - 1, :], PV).then_inc(ctx_evac, 1)

            def body(g, r, t):
                for s in range(KT):
                    exp(g, s)
                    if s == 0:
                        if not is_first(g):
                            evacuate(g, r, t)
                        if is_int(g, NG - 2):
                            act.wait_ge(ld_wo, 16)
                    if wo_part(g, s):
                        nc.scalar.copy(wo_hl[:, 0, wo_part(g, s)], wo_raw[:, wo_part(g, s)]).then_inc(wo_hi, 1)
                    for what, i in PLAN[2 * s] + PLAN[2 * s + 1]:
                        if what in ("k", "q") and has(g, what):
                            hi(g, what, i)
                    if s == 7 and r == 1 and more_weights(t):
                        split_w_hi(t + 2)
                    for b, n in splits(g, s):
                        o_hi_split(b, n)

            def o_hi_split(b, n):
                act.wait_ge(norm_done, 2 * n + b + 1)
                nc.scalar.copy(o_split(b, n)[0], ctxT[:, b, n, :]).then_inc(o_hi, 1)

            iterations(act, body)
            evacuate(NG, 0, NT)
            o_hi_split(1, NT - 1)

        @block.vector
        def _(dve):
            def split_w_lo(t):
                dve.wait_ge(w_hi, t + 1)
                nc.vector.tensor_tensor(wT[:, 1], wraw[:], wT[:, 0].bitcast(fp32), ALU.subtract).then_inc(w_lo, 1)

            def transposed_lo(u):
                dve.wait_ge(tr_hi, u + 1)
                t, grp, c = (cT, u // DC, u % DC) if u < CU else (xT, (u - CU) // DC, u % DC)
                hi, lo = [t[:, i, c, BANK * grp:BANK * grp + BANK] for i in range(2)]
                if u < CU:
                    nc.vector.tensor_tensor(lo, transposed(u), hi.bitcast(fp32), ALU.subtract).then_inc(tr_lo, 1)
                else:
                    nc.vector.scalar_tensor_tensor(out=lo, in0=transposed(u), scalar=nw[:, c:c + 1],
                                                   in1=hi.bitcast(fp32), op0=ALU.mult,
                                                   op1=ALU.subtract).then_inc(tr_lo, 1)

            for u in range(4):
                if u == 2:
                    split_w_lo(0)
                transposed_lo(u)

            def split_wv_lo():
                for c in range(DC):
                    dve.wait_ge(wv_hi, c + 1)
                    nc.vector.tensor_tensor(wv_hl[1][:, c], wv_raw[:, c], wv_hl[0][:, c].bitcast(fp32),
                                            ALU.subtract).then_inc(wv_lo, 1)

            split_wv_lo()
            for u in (4, 5):
                transposed_lo(u)

            def lo(g, what, i=0):
                bank, _ = aux(g, what, i)
                t = khl if what == "k" else qhl
                cols = slice(BANK * i, BANK * i + BANK)
                dve.wait_ge(hi_done, 3 * (g + 2) + PROJECTIONS.index((what, i)) + 1)
                nc.vector.tensor_tensor(t[:, 1, cols], bank, t[:, 0, cols].bitcast(fp32),
                                        ALU.subtract).then_inc(aux_free, 1)

            def reduce(g, i):
                bank, u = aux(g, "max", i)
                dve.wait_ge(aux_ready, u + 1)
                j, k, q = max_unit(i)
                nc.vector.reduce_max(mpart[:, QT * j + q, k:k + 1], bank, AX.X).then_inc(aux_free, 1)

            def combine(g):
                dve.wait_ge(aux_free, aux(g, "max", NMAX - 1)[1] + 1)
                nc.vector.reduce_max(mcol[:], mpart[:], AX.X).then_inc(mcol_ready, 1)

            def spread(g, r):
                bank, u = aux(g, "maxT")
                dve.wait_ge(aux_ready, u + 1)
                dst = qst[DK:DK + ROWS, r, 1].rearrange("p j (n q) -> p (j n) q", q=P)
                src = bank[0:ROWS, 0:P].unsqueeze(1).to_broadcast([ROWS, ROWS, P])
                nc.vector.tensor_tensor(dst, src, mask[:], ALU.mult).then_inc(aux_free, 1)

            for i in range(KH):
                lo(-2, "k", i)

            for v in range(2 * NC):
                if v % 2 == 1:
                    dve.wait_ge(v_ready, v + 1)
                    if v >= 4:
                        dve.wait_ge(st_v[v % 4], 16 * (v // 4))
                    nc.vector.tensor_copy(stage[:, v % 4], ps[:, v % 4, :]).then_inc(v_dve, 1)
                for what, i in AFTER_V[v]:
                    if what == "norm":
                        dve.wait_ge(rstd_done, 1)
                        for n in range(NX):
                            nc.vector.tensor_scalar(xn[:, n], xres[:, n], rstd[:, n:n + 1], None,
                                                    ALU.mult).then_inc(xn_done, 1)
                    elif what == "T":
                        transposed_lo(i)
                    elif what == "q":
                        lo(i, "q")
                    elif what == "max":
                        reduce(-1, i)
                        if i == NMAX - 1:
                            combine(-1)
                    elif what == "k":
                        for h in range(KH):
                            lo(i, "k", h)
            dve.wait_ge(const, 4)
            dve.wait_ge(rows_q, 1)
            spread(-1, 0)
            lo(-1, "q")
            split_w_lo(1)

            def add(g):
                dve.wait_ge(p_ready, KT * (g + 1))
                dve.wait_ge(add_pool, POOL_ADDS * (g + 1))
                nc.vector.tensor_tensor(acc[:], accp[:], probs[:, (KT - 1) % NP], ALU.add).then_inc(sum_done, 1)

            def invert(unit):
                bank, u = unit
                dve.wait_ge(aux_ready, u + 1)
                nc.vector.reciprocal(rec[:], bank).then_inc(aux_free, 1)

            def normalise(g, inverted, b, n):
                dve.wait_ge(ctx_evac, g)
                dve.wait_ge(aux_free, inverted)
                nc.vector.tensor_tensor(ctxT[:, b, n, :], ctxT[:, b, n, :], rec[:], ALU.mult).then_inc(norm_done, 1)

            def o_lo_split(b, n):
                dve.wait_ge(o_hi, b * NT + n + 1)
                h, l = o_split(b, n)
                nc.vector.tensor_tensor(l, ctxT[:, b, n, :], h.bitcast(fp32), ALU.subtract).then_inc(o_lo, 1)

            def residual(n, unit):
                bank, u = unit
                dve.wait_ge(aux_ready, u + 1)
                if n >= 4:
                    dve.wait_ge(st_o[n % 4], 16 * (n // 4))
                nc.vector.tensor_tensor(osb[:, n % 4], bank[:, 0:D], xres[:, n], ALU.add).then_inc(o_res, 1)

            def body(g, r, t):
                last = is_last(g)
                if r == 0 and not is_first(g) and more_weights(t - 1):
                    split_w_lo(t + 1)
                for s in range(KT):
                    for what, i in PLAN[2 * s] + PLAN[2 * s + 1]:
                        if not has(g, what):
                            continue
                        if what == "max":
                            reduce(g, i)
                            if i == NMAX - 1:
                                combine(g)
                        elif what == "den":
                            unit = tail(DEN_PREV) if last else aux(g, "den")
                            invert(unit)
                        elif what == "maxT":
                            spread(g, 1 - r)
                            add(g)
                        else:
                            lo(g, what, i)
                    if s == 2 and not is_first(g):
                        normalise(g, unit[1] + 1, 1 - r, t + r - 1)
                    for b, n in splits(g, s):
                        o_lo_split(b, n)
                    if last and s == 7:
                        residual(0, tail(WO0))

            iterations(dve, body)
            add(NG - 1)
            for i in range(WO0 + 1, TAIL_UNITS):
                if i == DEN_LAST:
                    invert(tail(i))
                    normalise(NG, DENS_FREE, 1, NT - 1)
                    o_lo_split(1, NT - 1)
                else:
                    residual(i - WO0 - (i > DEN_LAST), tail(i))

        @block.tensor
        def _(pe):
            mm = nc.tensor.matmul

            pe.wait_ge(const, 1)
            def transposes(u):
                src, grp, c = (craw, u // DC, u % DC) if u < CU else (xn, (u - CU) // DC, u % DC)
                if u < CU:
                    pe.wait_ge(ld_c[grp], 16)
                else:
                    pe.wait_ge(xn_done, NX)
                if u >= 6:
                    pe.wait_ge(tr_lo, u - 1)
                for i in range(4):
                    last = nc.tensor.transpose(transposed(u)[:, P * i:P * i + P],
                                               src[:, 4 * grp + i, P * c:P * c + P], ident[:])
                last.then_inc(tr_ready, 1)

            for u in range(4):
                transposes(u)

            def aux_wait(u):
                if not (isinstance(u, int) and u < 3):
                    pe.wait_ge(aux_free, u - 2)

            def split_product(bank, lhs, rhs, chunks, before_last=None):
                terms = [(h, l, c) for c in range(chunks) for h, l in ((0, 0), (0, 1), (1, 0))]
                for i, (h, l, c) in enumerate(terms):
                    if before_last and i == len(terms) - 3:
                        pe.wait_ge(*before_last)
                    last = mm(bank, lhs(h, c), rhs(l, c), start=(i == 0), stop=(i == len(terms) - 1))
                return last

            def project(g, what, i, b):
                bank, u = aux(g, what, i)
                aux_wait(u)
                m = 1 if what == "k" else 0
                src, col = (cT, KV * b + BANK * i) if what == "k" else (xT, Q * b)
                split_product(bank, lambda h, c: wT[:, h, m, c], lambda h, c: src[:, h, c, col:col + BANK],
                              DC).then_inc(aux_ready, 1)

            def wait_stacks(g, i):
                j, k, q = max_unit(i)
                if q == 0 and k == 0:
                    pe.wait_ge(st_q[j], STACKED * (g + 2))
                    if j == 0:
                        pe.wait_ge(st_k0, STACKED_K0 * (g + 2))
                elif q == 0:
                    pe.wait_ge(st_k1[j], STACKED * (g + 2))

            def approx_scores(g, r, i):
                bank, u = aux(g, "max", i)
                j, k, q = max_unit(i)
                wait_stacks(g, i)
                aux_wait(u)
                mm(bank, qst[:, r, 0, j, P * q:P * q + P], kst[:, r, 0, j, BANK * k:BANK * k + BANK],
                   start=True, stop=True).then_inc(aux_ready, 1)

            def max_rows(g):
                bank, u = aux(g, "maxT")
                pe.wait_ge(mcol_ready, g + 2)
                aux_wait(u)
                nc.tensor.transpose(bank[0:ROWS, 0:P], mcol[:], ident[:]).then_inc(aux_ready, 1)

            def scores(g, r, s):
                buf = S[s % 2]
                if not (is_first(g) and s < 2):
                    pe.wait_ge(p_ready, KT * g + s - 1)
                keys = slice(P * s, P * s + P)
                for j in range(2):
                    mm(buf[:, j], kst[:, r, 0, j, keys], qst[:, r, 0, j], start=True, stop=False)
                if s == 0:
                    pe.wait_ge(aux_free, aux(g - 1, "maxT")[1] + 1)
                    if is_first(g):
                        pe.wait_ge(rows_k0, 2)
                    if isinstance(g, int) and g == 1:
                        pe.wait_ge(rows_k1, 2)
                for j in range(2):
                    last = mm(buf[:, j], kst[:, r, 1, j, keys], qst[:, r, 1, j], start=False, stop=True)
                last.then_inc(s_ready, 1)

            def values(g, r, s, t):
                pe.wait_ge(p_ready, KT * g + s + 1)
                if s == 0:
                    pe.wait_ge(ld_v[r], 16 * (t + 1))
                    if not is_first(g):
                        pe.wait_ge(ctx_evac, g)
                for j in range(2):
                    rows = slice(DK * j, DK * j + DK)
                    last = mm(PV[rows, :], vals[:, r, s, rows], probs[:, s % NP, j],
                              start=(s == 0), stop=(s == KT - 1))
                last.then_inc(pv_done, 1)

            def denominators(g, unit):
                bank, u = unit
                pe.wait_ge(sum_done, g)
                if isinstance(g, int) and g == NG:
                    tail_wait(DEN_LAST)
                else:
                    aux_wait(u)
                for j in range(2):
                    last = mm(bank[DK * j:DK * j + DK, :], ones[:], acc[:, j], start=True, stop=True)
                last.then_inc(aux_ready, 1)

            def tail_wait(i):
                if i - 3 <= DEN_PREV:
                    pe.wait_ge(aux_free, TAIL + i - 2)
                elif i - 3 == DEN_LAST:
                    pe.wait_ge(aux_free, DENS_FREE)
                else:
                    pe.wait_ge(o_res, i - 3 - WO0 + 1 - (i - 3 > DEN_LAST))

            def output(n, i):
                bank, _ = tail(i)
                tail_wait(i)
                if n == 0:
                    pe.wait_ge(wo_lo, 1)
                    pe.wait_ge(o_lo, NT)
                if n == QT:
                    pe.wait_ge(o_lo, 2 * NT - 1)
                b, rows = n // QT, slice(P * (n % QT), P * (n % QT) + P)
                split_product(bank[:, 0:D], lambda h, c: o_split(b, c)[h][:, rows], lambda l, c: wo_hl[:, l, c],
                              NT, (o_lo, 2 * NT) if n == QT else None).then_inc(aux_ready, 1)

            pe.wait_ge(w_lo, 1)
            for i in range(KH):
                pe.wait_ge(tr_lo, DC * (i + 1))
                project(-2, "k", i, 0)
            for u in (4, 5):
                transposes(u)
            pe.wait_ge(wv_lo, DC)
            for v in range(2 * NC):
                if v >= 4:
                    pe.wait_ge(v_act if v % 2 == 0 else v_dve, (v - 4) // 2 + 1)
                if v == NC // 2:
                    pe.wait_ge(tr_lo, CU)
                rows = slice(P * (v % NC), P * (v % NC) + P)
                cols = slice(BANK * (v // NC), BANK * (v // NC) + BANK)
                split_product(ps[:, v % 4, :], lambda h, c: cT[:, h, c, rows], lambda l, c: wv_hl[l][:, c, cols],
                              DC).then_inc(v_ready, 1)
                for what, i in AFTER_V[v]:
                    if what == "T":
                        transposes(i)
                    elif what == "q":
                        pe.wait_ge(tr_lo, CU + XU)
                        project(i, "q", 0, 0)
                    elif what == "max":
                        approx_scores(-1, 0, i)
                    elif what == "k":
                        for h in range(KH):
                            project(i, "k", h, 1)
            max_rows(-1)
            project(-1, "q", 0, 1)
            pe.wait_ge(v_act, NC)
            pe.wait_ge(v_dve, NC)

            def body(g, r, t):
                def units(todo):
                    for what, i in todo:
                        if not has(g, what):
                            continue
                        if what == "max":
                            approx_scores(g, 1 - r, i)
                        elif what == "maxT":
                            max_rows(g)
                        elif what == "den":
                            denominators(g, tail(DEN_PREV) if is_last(g) else aux(g, "den"))
                        else:
                            pe.wait_ge(w_lo, t + 2)
                            project(g, what, i, r)

                for s in range(KT):
                    scores(g, r, s)
                    units(PLAN[2 * s])
                    if s == KT - 1 and is_int(g, NG - 2):
                        units(PLAN[2 * s + 1])
                    if s > 0:
                        values(g, r, s - 1, t)
                    elif not is_first(g):
                        values(g - 1, 1 - r, KT - 1, t + r - 1)
                    if not (s == KT - 1 and is_int(g, NG - 2)):
                        units(PLAN[2 * s + 1])
                    if is_last(g) and s == 6:
                        output(0, WO0)
            iterations(pe, body)
            output(1, WO0 + 1)
            values(NG - 1, 1, KT - 1, NT - 1)
            for i in range(DEN_LAST, TAIL_UNITS):
                if i == DEN_LAST:
                    denominators(NG, tail(i))
                else:
                    output(i - WO0 - 1, i)


_INS = ['x', 'ctx_1024', 'L0_xattn_wq', 'L0_xattn_wk', 'L0_xattn_wv', 'L0_xattn_wo', 'L0_xattn_norm_w']


def kernel(**inputs):
    import numpy as _np
    import concourse.bacc as _bacc
    from concourse import mybir as _mybir
    from concourse.bass_utils import run_bass_kernel_spmd as _run

    nc = _bacc.Bacc("TRN2", target_bir_lowering=False, num_devices=1)
    arrays, args = {}, []
    for name in _INS:
        a = _np.ascontiguousarray(inputs[name])
        arrays[f"in_{name}"] = a
        args.append(nc.dram_tensor(f"in_{name}", a.shape, _mybir.dt.from_np(a.dtype), kind="ExternalInput").ap())
    args.append(nc.dram_tensor("out_0", tuple(inputs['x'].shape), _mybir.dt.float32, kind="ExternalOutput").ap())
    cross_attention_program(nc, *args)
    r = _run(nc, [arrays], core_ids=[0])
    return r.results[0]["out_0"]
```
